# Optimizing a Trainium2 kernel written in Bass

```python
import numpy as np
import jax
import jax.numpy as jnp

def _softmax(x, axis=-1):
    return jax.nn.softmax(x, axis=axis)
def _gelu(x):
    return jax.nn.gelu(x, approximate=True)
def _silu(x):
    return jax.nn.silu(x)
def _sigmoid(x):
    return jax.nn.sigmoid(x)
def _layernorm(x, axis=-1, eps=1e-5):
    m = jnp.mean(x, axis=axis, keepdims=True)
    v = jnp.var(x, axis=axis, keepdims=True)
    return (x - m) / jnp.sqrt(v + eps)
def _scatter_add(tgt, idx, src, axis=0):
    return tgt.at[idx].add(src)
def _segment_sum(src, seg, n):
    return jax.ops.segment_sum(src, seg, n)

kernel_name = 'mk_conv_preact_d2_conv_nchw32_56c3dd'

def setup_inputs(seed: int = 0):
    np.random.seed(seed)
    _w = jnp.asarray
    def _rec_inputs():
        import jax
        import jax.numpy as jnp
        _gk = jax.random.key(seed)
        x = 1.508e-05 + 1 * jax.random.normal(jax.random.fold_in(_gk, 1), (8, 32, 512, 512), jnp.float32)
        return x
    x = _rec_inputs()
    def _L0_conv_setup():
        import jax, jax.numpy as jnp
        import numpy as np
        LEVELS = 3

        def _wavelet_pyramid(x, levels=LEVELS):
            B, C, H, W = x.shape
            k1 = jnp.array([0.25, 0.5, 0.25], dtype=x.dtype)
            K = jnp.outer(k1, k1)[None, None]
            result = x
            for level in range(levels):
                sh, sw = (H // 2 ** level, W // 2 ** level)
                if min(sh, sw) <= 2:
                    break
                temp = result[:, :, :sh, :sw].reshape(B * C, 1, sh, sw)
                approx = jax.lax.conv_general_dilated(temp, K, window_strides=(1, 1), padding='SAME', dimension_numbers=('NCHW', 'OIHW', 'NCHW'))
                down = approx[:, :, ::2, ::2][:, :, :sh // 2, :sw // 2]
                result = result.at[:, :, :sh // 2, :sw // 2].set(down.reshape(B, C, sh // 2, sw // 2))
            return result
        key = jax.random.key(seed)
        x = jax.random.normal(key, (8, 32, 512, 512), dtype=jnp.float32)
        return {'x': x}
    _L0_conv_all = _L0_conv_setup()
    _L0_conv_in = {k: v for k, v in _L0_conv_all.items() if k in ()}
    del _L0_conv_all

    def _L1_conv_setup():
        import jax, jax.numpy as jnp
        import numpy as np
        B, C_IN, H, W = (16, 32, 256, 256)
        C_OUT, KH, KW = (32, 3, 3)
        STRIDE = (1, 1)
        PADDING = (1, 1)
        key = jax.random.key(seed)
        kx, kw = jax.random.split(key)
        x = jax.random.normal(kx, (B, C_IN, H, W), dtype=jnp.float32)
        fan_in = C_IN * KH * KW
        bound = float(np.sqrt(6.0 / fan_in))
        weight = jax.random.uniform(kw, (C_OUT, C_IN, KH, KW), dtype=jnp.float32, minval=-bound, maxval=bound)
        bias = jnp.zeros((C_OUT,), dtype=jnp.float32)
        return {'x': x, 'weight': weight, 'bias': bias}
    _L1_conv_all = _L1_conv_setup()
    _L1_conv_in = {k: v for k, v in _L1_conv_all.items() if k in ('weight', 'bias', )}
    del _L1_conv_all

    return {
        "x": x,
        "L1_conv_weight": _L1_conv_in["weight"],
        "L1_conv_bias": _L1_conv_in["bias"],
    }

def reference(x, L1_conv_weight, L1_conv_bias):
    import jax
    import jax.numpy as jnp
    def _L0_conv_ref(x):
        import jax, jax.numpy as jnp
        import numpy as np
        LEVELS = 3

        def _wavelet_pyramid(x, levels=LEVELS):
            B, C, H, W = x.shape
            k1 = jnp.array([0.25, 0.5, 0.25], dtype=x.dtype)
            K = jnp.outer(k1, k1)[None, None]
            result = x
            for level in range(levels):
                sh, sw = (H // 2 ** level, W // 2 ** level)
                if min(sh, sw) <= 2:
                    break
                temp = result[:, :, :sh, :sw].reshape(B * C, 1, sh, sw)
                approx = jax.lax.conv_general_dilated(temp, K, window_strides=(1, 1), padding='SAME', dimension_numbers=('NCHW', 'OIHW', 'NCHW'))
                down = approx[:, :, ::2, ::2][:, :, :sh // 2, :sw // 2]
                result = result.at[:, :, :sh // 2, :sw // 2].set(down.reshape(B, C, sh // 2, sw // 2))
            return result
        return _wavelet_pyramid(x, LEVELS)

    def _L1_conv_ref(x, weight, bias):
        import jax, jax.numpy as jnp
        import numpy as np
        B, C_IN, H, W = (16, 32, 256, 256)
        C_OUT, KH, KW = (32, 3, 3)
        STRIDE = (1, 1)
        PADDING = (1, 1)
        out = jax.lax.conv_general_dilated(x, weight, window_strides=STRIDE, padding=[(PADDING[0], PADDING[0]), (PADDING[1], PADDING[1])], dimension_numbers=('NCHW', 'OIHW', 'NCHW'))
        return out + bias[None, :, None, None]

    def _gn(v, G=16, eps=1e-5):
        B_, C_, H_, W_ = v.shape
        g = v.reshape(B_, G, C_ // G, H_, W_)
        m = jnp.mean(g, axis=(2, 3, 4), keepdims=True)
        s = jnp.var(g, axis=(2, 3, 4), keepdims=True)
        return ((g - m) / jnp.sqrt(s + eps)).reshape(v.shape)

    def _ln_c(v, eps=1e-6):
        m = jnp.mean(v, axis=1, keepdims=True)
        s = jnp.var(v, axis=1, keepdims=True)
        return (v - m) / jnp.sqrt(s + eps)

    def _ln_t(v, eps=1e-5):
        m = jnp.mean(v, axis=-1, keepdims=True)
        s = jnp.var(v, axis=-1, keepdims=True)
        return (v - m) / jnp.sqrt(s + eps)

    def _to_tokens(v):
        B_, C_, H_, W_ = v.shape
        return v.reshape(B_, C_, H_ * W_).transpose(0, 2, 1)
    def _from_tokens(t, like):
        B_, C_, H_, W_ = like.shape
        return t.transpose(0, 2, 1).reshape(B_, C_, H_, W_)

    x = x + _L0_conv_ref(_gn(x))
    x = x + _L1_conv_ref(_gn(x), L1_conv_weight, L1_conv_bias)
    return x


_drawn_inputs = setup_inputs


def setup_inputs(seed=0):
    import zlib

    import numpy as np

    out = dict(_drawn_inputs(seed))
    spreads = {'L1_conv_bias': (0.0, 0.1)}
    factors = {}
    for name, (base, spread) in spreads.items():
        noise = np.random.default_rng([zlib.crc32(name.encode()), seed]).standard_normal(out[name].shape)
        drawn = base * np.exp(spread * noise) if base else spread * noise
        out[name] = jnp.asarray(drawn.astype(out[name].dtype))
    for name, factor in factors.items():
        out[name] = (out[name] * factor).astype(out[name].dtype)
    return out
```

```python
from contextlib import ExitStack

import numpy as np

import concourse.bass as bass
from concourse import mybir

ALU = mybir.AluOpType
ACT = mybir.ActivationFunctionType
AX = mybir.AxisListType
F32 = mybir.dt.float32
F32R = mybir.dt.float32r
I32 = mybir.dt.int32

P = 128
Q = 4
EPS = 1e-5
PAD = 2
GROUP = 4
LEVELS = 3
E0 = (0.75, 0.625, 0.5625)
RSQRT_SEED = 0x5F3759DF
NEWTON_STEPS = 4
CHUNK = 4
MCHUNK = 8
K_LOWER, K_TOP, K_REGION, K_EDGE = 0, 1, 2, 7


def group_norm_pyramid_conv(nc, x, w_taps, bias, same_group, eye, shape_consts, out):
    B, C, H, W = x.shape
    assert C * Q == P and H == W and w_taps.shape[0] == C
    HW4 = H // Q
    N1 = HW4 // CHUNK
    WQ = W // 2
    LR = [HW4 >> (l + 1) for l in range(LEVELS)]
    LW = [W >> (l + 1) for l in range(LEVELS)]
    N2 = [r // MCHUNK for r in LR]
    NM = sum(N2)
    NA = N1 + NM
    assert NA % 2 == 0 and all(n % 2 == 0 for n in N2) and N1 % 2 == 0
    GR = GROUP * Q
    G = H // GR
    GQ = G // 2
    WP = W + 2
    GN = float(2 * H * W)
    UNIT = float(HW4 * WQ)
    SLOT = CHUNK * (W + 2 * PAD)
    YSTORES = sum(N2[:1]) + 2
    XSTAT_AT, YSTAT_AT = G - 14, G - 4

    y_quarter = nc.dram_tensor("y_quarter", (B, C, H // 2, WQ), F32, kind="Internal").ap()

    with ExitStack() as ctx:
        def sb(name, shape, dt=F32):
            return ctx.enter_context(nc.sbuf_tensor(name, shape, dt))

        def sem(name):
            return ctx.enter_context(nc.semaphore(name))

        xa = sb("xa", [P, 2, SLOT])
        xlast = sb("xlast", [P, W + PAD])
        hblur = sb("hblur", [P, 5 * WQ])
        level = [sb(f"level{l}", [P, LR[l], LW[l] + PAD]) for l in range(LEVELS)]
        xstats = sb("xstats", [P, 2, N1 * 2, 6])
        ystats = [sb(f"ystats{k}", [P, n, 6]) for k, n in enumerate((16, 16, 4, 4, 2))]
        moments = sb("moments", [P, 7, 2])
        small = sb("small", [P, 64])
        consts = sb("consts", [P, shape_consts.shape[1]])
        groups = sb("groups", [P, P])
        eyes = sb("eyes", [P, P])
        scal = sb("scal", [P, B, 8])
        norm_now = sb("norm_now", [P, 4])
        shift_now = sb("shift_now", [P, 2])
        raw = sb("raw", [P, 2, GROUP, W])
        high = sb("high", [P, 2 * GROUP, WP], F32R)
        low = sb("low", [P, 2 * GROUP, WP], F32R)
        halo = sb("halo", [P, 2, GROUP, WP], F32R)
        zeros = sb("zeros", [C, WP], F32R)
        outs = sb("outs", [P, 2, GROUP, W])
        w_high = sb("w_high", [P, 3, P], F32R)
        w_low = sb("w_low", [P, 3, P], F32R)
        wt_high = sb("wt_high", [P, 3, P], F32R)
        wt_low = sb("wt_low", [P, 3, P], F32R)
        w_centre = sb("w_centre", [P, P])
        biases = sb("biases", [P, 1])
        spare = sb("spare", [C, 4])
        w_sum = sb("w_sum", [P, P])
        sums = ctx.enter_context(nc.psum_tensor("sums", [P, 2, GROUP, W], F32))

        consts_in = sem("consts_in")
        weights_zeroed = sem("weights_zeroed")
        weights_in = sem("weights_in")
        weights_split = sem("weights_split")
        pads_zeroed = sem("pads_zeroed")
        conv_zeroed = sem("conv_zeroed")
        xa_in = [sem(f"xa_in{s}") for s in range(2)]
        xa_free = [sem(f"xa_free{s}") for s in range(2)]
        xlast_in = sem("xlast_in")
        xlast_free = sem("xlast_free")
        dve = sem("dve")
        y1_ready = sem("y1_ready")
        y23_ready = sem("y23_ready")
        y1_stored = sem("y1_stored")
        y2_stored = sem("y2_stored")
        y_stored = sem("y_stored")
        partial_ready = sem("partial_ready")
        total_ready = sem("total_ready")
        total_read = sem("total_read")
        scal_ready = sem("scal_ready")
        w_sum_ready = sem("w_sum_ready")
        centre_high_ready = sem("centre_high_ready")
        centre_ready = sem("centre_ready")
        raw_in = [sem(f"raw_in{s}") for s in range(2)]
        norm_now_ready = sem("norm_now_ready")
        shift_now_ready = sem("shift_now_ready")
        normed = sem("normed")
        high_ready = sem("high_ready")
        low_ready = sem("low_ready")
        above_in = [sem(f"above_in{s}") for s in range(2)]
        below_in = [sem(f"below_in{s}") for s in range(2)]
        main_done = sem("main_done")
        sums_ready = sem("sums_ready")
        sums_read = [sem(f"sums_read{s}") for s in range(2)]
        out_stored = [sem(f"out_stored{s}") for s in range(2)]

        wm = [level[0][:, 3 * k:3 * k + 3, 0:P] for k in range(2)]
        LEFT, RIGHT = slice(PAD, PAD + WQ), slice(PAD + WQ, PAD + W)

        def x_rows(slot):
            return xa[:, slot, :].rearrange("p (r w) -> p r w", r=CHUNK)

        def m_rows(slot, width):
            return xa[:, slot, :].rearrange("p (r w) -> p r w", r=MCHUNK)[:, :, PAD:PAD + width]

        def store_y1(sp, i, k):
            sp.wait_ge(y1_ready, i * N2[0] + (k + 1))
            sp.dma_start(y_quarter[i].rearrange("c (q r) w -> (c q) r w", q=Q)
                         [:, MCHUNK * k:MCHUNK * k + MCHUNK, :],
                         level[0][:, MCHUNK * k:MCHUNK * k + MCHUNK, PAD:PAD + WQ]
                         ).then_inc(y1_stored, 16)

        def store_level(sp, i, l, done):
            for q in reversed(range(Q)):
                sp.dma_start(y_quarter[i, :, q * LR[l]:(q + 1) * LR[l], 0:LW[l]],
                             level[l][q:P:Q, :, PAD:PAD + LW[l]]).then_inc(done, 16)

        block = ctx.enter_context(nc.Block())

        @block.sync
        def _(sp):
            for k, done in enumerate((y1_stored, y_stored)):
                sp.dma_start(spare[:, k:k + 1], bias.rearrange("(c o) -> c o", o=1)).then_inc(done, 16)
            sp.dma_start(consts[:], shape_consts).then_inc(consts_in, 16)
            sp.dma_start(groups[:], same_group).then_inc(consts_in, 16)
            sp.dma_start(eyes[:], eye).then_inc(consts_in, 16)
            for r in range(Q):
                sp.dma_start(biases[r:P:Q, :], bias.rearrange("(c o) -> c o", o=1)).then_inc(consts_in, 16)
            sp.wait_ge(weights_zeroed, 1)
            for r in range(Q):
                for o in range(Q):
                    if 0 <= r - o + 1 < 3:
                        sp.dma_start(wm[0][r:P:Q, :, C * o:C * o + C],
                                     w_taps[:, r - o + 1]).then_inc(weights_in, 16)
            for part in range(4):
                ky, o = (0, 0) if part % 2 == 0 else (2, Q - 1)
                sp.dma_start(wm[1][C * part:C * part + C, :, C * o:C * o + C],
                             w_taps[:, ky]).then_inc(weights_in, 16)

            with sp.Fori(0, B) as i:
                rows = x[i].rearrange("c (q r) w -> (c q) r w", q=Q)
                chunks = x[i].rearrange("c (q k s r) w -> (c q) k s r w", q=Q, s=2, r=CHUNK)
                sp.wait_ge(xlast_free, i + 1)
                sp.dma_start(xlast[:, PAD:PAD + W], rows[:, HW4 - 1, :]).then_inc(xlast_in, 16)
                with sp.Fori(0, N1 // 2) as k:
                    for s in range(2):
                        sp.wait_ge(xa_free[s], i * (NA // 2) + k + 1)
                        sp.dma_start(x_rows(s)[:, :, PAD:PAD + W],
                                     chunks[:, bass.ds(k, 1), s].rearrange("p o r w -> p (o r) w")
                                     ).then_inc(xa_in[s], 16 * Q)
                done = N1
                for l in range(LEVELS):
                    part = x[i, :, 0:H >> (l + 1), 0:LW[l]].rearrange("c (q r) w -> c q r w", q=Q)
                    for k in range(N2[l]):
                        s = k % 2
                        sp.wait_ge(xa_free[s], i * (NA // 2) + (done // 2 + k // 2 + 1))
                        for q in reversed(range(Q)):
                            sp.dma_start(m_rows(s, LW[l])[q:P:Q],
                                         part[:, q, MCHUNK * k:MCHUNK * k + MCHUNK, :]
                                         ).then_inc(xa_in[s], 16)
                        if l == 0 and k >= 2:
                            store_y1(sp, i, k - 2)
                    if l == 0:
                        store_y1(sp, i, N2[0] - 2)
                        store_y1(sp, i, N2[0] - 1)
                    done += N2[l]
                sp.wait_ge(y1_stored, i * (16 * N2[0]) + 16 * (N2[0] + 1))
                sp.wait_ge(y23_ready, i * 2 + 1)
                store_level(sp, i, 1, y2_stored)
                sp.wait_ge(y23_ready, i * 2 + 2)
                sp.wait_ge(y2_stored, i * (16 * Q) + 16 * Q)
                store_level(sp, i, 2, y_stored)
            sp.wait_ge(y_stored, 16 * Q * B + 16)

        @block.vector
        def _(v):
            steps = [0, 0]

            def link(ins):
                steps[1] += 1
                ins.then_inc(dve, 1)
                v.wait_ge(dve, steps[0] + steps[1])

            one = shape_consts.shape[1] - 1

            def col(n, width=1):
                return small[:, n:n + width]

            def carry_wait():
                nc.vector.memset(col(63), 0.0)

            def blur(src, n, width, dst, between=lambda k: None):
                def link(ins, k):
                    steps[1] += 1
                    ins.then_inc(dve, 1)
                    between(k)
                    v.wait_ge(dve, steps[0] + steps[1])

                h = hblur[:, 0:(n + 1) * width].rearrange("p (r w) -> p r w", w=width)
                left, mid = src[:, :, 1:1 + 2 * width:2], src[:, :, 2:2 + 2 * width:2]
                right = src[:, :, 3:2 + 2 * width:2]
                link(nc.vector.tensor_tensor(h[:, 1:n + 1, :], left, right, ALU.add), 0)
                link(nc.vector.scalar_tensor_tensor(out=h[:, 1:n + 1, :], in0=mid, scalar=2.0,
                                                    in1=h[:, 1:n + 1, :], op0=ALU.mult, op1=ALU.add), 1)
                link(nc.vector.tensor_tensor(dst, h[:, 0:n - 1:2, :], h[:, 2:n + 1:2, :], ALU.add), 2)
                nc.vector.scalar_tensor_tensor(out=dst, in0=h[:, 1:n:2, :], scalar=2.0, in1=dst,
                                               op0=ALU.mult, op1=ALU.add)
                link(nc.vector.tensor_copy(h[:, 0, :], h[:, n, :]), 3)

            def blur_last_row(src, width):
                shift = [max(p - 1, 0) for p in range(32)]
                carry_wait()
                link(nc.vector.stream_shuffle(src, src, shift))
                h = hblur[:, 0:width]
                link(nc.vector.tensor_tensor(h, src[:, 1:1 + 2 * width:2], src[:, 3:2 + 2 * width:2], ALU.add))
                link(nc.vector.scalar_tensor_tensor(out=h, in0=src[:, 2:2 + 2 * width:2], scalar=2.0,
                                                    in1=h, op0=ALU.mult, op1=ALU.add))
                link(nc.vector.tensor_scalar(h, h, consts[:, K_TOP:K_TOP + 1], None, ALU.mult))

            def rsqrt(dst, var, t0, t1):
                link(nc.vector.tensor_scalar(t0.bitcast(I32), var.bitcast(I32), 1, None,
                                             ALU.arith_shift_right))
                link(nc.vector.tensor_scalar(dst.bitcast(I32), t0.bitcast(I32), -1.0,
                                             float(RSQRT_SEED), ALU.mult, ALU.add))
                for _ in range(NEWTON_STEPS):
                    link(nc.vector.scalar_tensor_tensor(out=t0, in0=dst, scalar=dst, in1=var,
                                                        op0=ALU.mult, op1=ALU.mult))
                    link(nc.vector.tensor_scalar(t1, t0, -0.5, 1.5, ALU.mult, ALU.add))
                    link(nc.vector.tensor_tensor(dst, dst, t1, ALU.mult))


            def total(n_done, mean, r, sigma):
                v.wait_ge(total_ready, n_done)
                nc.vector.tensor_scalar(col(2, 2), sums[:, 0, 0, 0:2], UNIT / GN, None,
                                        ALU.mult).then_inc(total_read, 1)
                v.wait_ge(total_read, n_done)
                link(nc.vector.tensor_copy(mean, col(2)))
                link(nc.vector.tensor_tensor(col(4), col(2), col(2), ALU.mult))
                link(nc.vector.tensor_tensor(col(4), col(3), col(4), ALU.subtract))
                link(nc.vector.tensor_scalar(col(4), col(4), 0.0, EPS, ALU.max, ALU.add))
                rsqrt(r, col(4), col(5), col(6))
                link(nc.vector.tensor_tensor(sigma, col(4), r, ALU.mult))

            nc.vector.memset(xlast[:], 0.0)
            for l in range(1, LEVELS):
                nc.vector.memset(level[l][:], 0.0)
            nc.vector.memset(xa[:], 0.0)
            nc.vector.memset(level[0][:], 0.0).then_inc(weights_zeroed, 1)
            v.wait_ge(weights_zeroed, 1)
            v.wait_ge(weights_in, 16 * 14)
            v.wait_ge(consts_in, 16 * (3 + Q))
            for fine, hi, lo in ((wm[0], w_high, w_low), (wm[1], wt_high, wt_low)):
                for kx in range(3):
                    f = fine[:, kx, :].rearrange("p (o c) -> p c o", o=Q)
                    h = hi[:, kx, :].rearrange("p (c o) -> p c o", o=Q)
                    l = lo[:, kx, :].rearrange("p (c o) -> p c o", o=Q)
                    link(nc.vector.tensor_copy(h, f))
                    link(nc.vector.tensor_tensor(l, f, h.bitcast(F32), ALU.subtract))
            link(nc.vector.tensor_scalar(wt_low[2 * C:P, :, :], wt_low[2 * C:P, :, :].bitcast(F32), 0.0, None, ALU.mult))
            link(nc.vector.tensor_copy(w_centre[:].rearrange("p (c o) -> p c o", o=Q),
                                       wm[0][:, 1, :].rearrange("p (o c) -> p c o", o=Q)))
            nc.vector.memset(level[0][:, 0:6, 0:PAD], 0.0).then_inc(weights_split, 1)
            v.wait_ge(weights_split, 1)
            nc.vector.memset(small[:, 0:16], 0.0).then_inc(xa_free[0], 1)
            nc.vector.memset(small[:, 16:32], 0.0).then_inc(xa_free[1], 1)
            nc.vector.memset(small[:, 32:64], 0.0).then_inc(xlast_free, 1)
            for s in range(2):
                v.wait_ge(xa_free[s], 1)
            v.wait_ge(xlast_free, 1)

            first = steps[1]
            with v.Fori(0, B) as i:
                base = i * STEPS_IMAGE + first
                steps[0], steps[1] = base, 0
                v.wait_ge(y1_stored, i * (16 * N2[0]) + 16)
                v.wait_ge(y_stored, i * (16 * Q) + 16)
                v.wait_ge(xlast_in, i * 16 + 16)
                blur_last_row(xlast[:, 0:PAD + W], WQ)
                before = steps[1]
                carry_wait()
                with v.Fori(0, N1 // 2) as k:
                    steps[0], steps[1] = base + k * STEPS_CHUNKS + before, 0
                    for s in range(2):
                        v.wait_ge(xa_in[s], i * (8 * NA * Q) + k * (16 * Q) + 16 * Q)

                        def stats(n):
                            half, pair = divmod(n, CHUNK // 2)
                            ins = nc.vector.bn_stats(
                                xstats[:, half, bass.ds(k * CHUNK + (s * CHUNK // 2 + pair), 1), :]
                                .rearrange("p o k -> p (o k)"),
                                x_rows(s)[:, 2 * pair:2 * pair + 2, (LEFT, RIGHT)[half]])
                            if n == CHUNK - 1:
                                ins.then_inc(xa_free[s], 1)

                        blur(x_rows(s), CHUNK, WQ,
                             level[0][:, bass.ds(k * CHUNK + s * CHUNK // 2, CHUNK // 2), PAD:PAD + WQ],
                             between=stats)
                    assert steps[1] == STEPS_CHUNKS, steps
                steps[0], steps[1] = base, before + STEPS_CHUNKS * (N1 // 2)
                v.wait_ge(xa_free[1], i * (NA // 2) + (N1 // 2 + 1))
                carry_wait()
                nc.vector.bn_aggr(moments[:, 0, :], xstats[:, 0, :, :])
                link(nc.vector.bn_aggr(moments[:, 1, :], xstats[:, 1, :, :]))
                mean, var = moments[:, 0:2, 0], moments[:, 0:2, 1]
                link(nc.vector.tensor_tensor(col(10, 2), mean, mean, ALU.mult))
                link(nc.vector.tensor_tensor(col(10, 2), col(10, 2), var, ALU.add))
                link(nc.vector.tensor_tensor(col(0), moments[:, 0, 0:1], moments[:, 1, 0:1], ALU.add))
                nc.vector.tensor_tensor(col(1), col(10), col(11), ALU.add).then_inc(partial_ready, 1)
                link(nc.vector.scalar_tensor_tensor(out=col(12), in0=moments[:, 0, 0:1],
                                                    scalar=consts[:, K_LOWER:K_LOWER + 1],
                                                    in1=moments[:, 1, 0:1], op0=ALU.mult, op1=ALU.add))
                link(nc.vector.scalar_tensor_tensor(out=col(13), in0=col(10),
                                                    scalar=consts[:, K_LOWER:K_LOWER + 1],
                                                    in1=col(11), op0=ALU.mult, op1=ALU.add))
                for l in range(1, LEVELS):
                    last = xlast[:, 0:PAD + LW[l - 1]]
                    link(nc.vector.tensor_copy(last[:, PAD:], level[l - 1][:, LR[l - 1] - 1, PAD:]))
                    blur_last_row(last, LW[l])
                    for k in range(LR[l - 1] // MCHUNK):
                        blur(level[l - 1][:, MCHUNK * k:MCHUNK * k + MCHUNK, :], MCHUNK, LW[l],
                             level[l][:, MCHUNK // 2 * k:MCHUNK // 2 * (k + 1), PAD:])
                total(i * 2 + 1, col(7), col(20), col(8))
                link(nc.vector.scalar_tensor_tensor(out=col(21), in0=col(7), scalar=-1.0, in1=col(20),
                                                    op0=ALU.mult, op1=ALU.mult))
                nc.vector.tensor_scalar(col(22), col(20), 1.0, None, ALU.add).then_inc(xlast_free, 1)
                v.wait_ge(xlast_free, i + 2)
                seen = N1 // 2
                edge = K_EDGE
                for l in range(LEVELS):
                    link(nc.vector.tensor_scalar(col(23), col(20), 16.0 ** -(l + 1), None, ALU.mult))
                    link(nc.vector.tensor_scalar(col(24), col(21), E0[l] - 1.0, None, ALU.mult))
                    link(nc.vector.tensor_tensor(col(24), col(24), consts[:, one:one + 1], ALU.mult))
                    for k in range(N2[l]):
                        s = k % 2
                        rows = slice(MCHUNK * k, MCHUNK * k + MCHUNK)
                        y = level[l][:, rows, PAD:]
                        xq = m_rows(s, LW[l])
                        v.wait_ge(xa_in[s], i * (8 * NA * Q) + 16 * Q * (seen + k // 2 + 1))
                        link(nc.vector.scalar_tensor_tensor(out=y, in0=y, scalar=col(23), in1=xq,
                                                            op0=ALU.mult, op1=ALU.add))
                        nc.vector.tensor_scalar(y, y, col(21), None, ALU.add).then_inc(xa_free[s], 1)
                        v.wait_ge(xa_free[s], i * (NA // 2) + (seen + k // 2 + 2))
                        ec = consts[:, edge + MCHUNK * k:edge + MCHUNK * k + MCHUNK].rearrange("p (r o) -> p r o", o=1)
                        last = nc.vector.scalar_tensor_tensor(out=y[:, :, 0:1], in0=ec, scalar=col(21),
                                                       in1=y[:, :, 0:1], op0=ALU.mult, op1=ALU.add)
                        if k == 0:
                            link(last)
                            last = nc.vector.tensor_scalar(y[:, 0, 1:], y[:, 0, 1:], col(24), None, ALU.add)
                        if l == 0:
                            last.then_inc(y1_ready, 1)
                            v.wait_ge(y1_ready, i * N2[0] + (k + 1))
                        else:
                            link(last)
                        if l < LEVELS - 1:
                            n = 512 // (LW[l] // 2)
                            for j in range(MCHUNK // n):
                                for half in range(2):
                                    last = nc.vector.bn_stats(
                                        ystats[2 * l + half][:, k * (MCHUNK // n) + j, :],
                                        y[:, n * j:n * j + n, half * LW[l] // 2:(half + 1) * LW[l] // 2])
                        else:
                            last = nc.vector.bn_stats(ystats[2 * l][:, k, :], y)
                    if l:
                        last.then_inc(y23_ready, 1)
                    seen += N2[l] // 2
                    edge += LR[l]
                v.wait_ge(y23_ready, i * 2 + 2)
                carry_wait()
                for k in range(5):
                    last = nc.vector.bn_aggr(moments[:, 2 + k, :], ystats[k][:])
                link(last)
                mean, var = moments[:, 2:7, 0], moments[:, 2:7, 1]
                weight = consts[:, K_REGION:K_REGION + 5]
                link(nc.vector.tensor_tensor(col(30, 5), mean, mean, ALU.mult))
                link(nc.vector.tensor_tensor(col(30, 5), col(30, 5), var, ALU.add))
                link(nc.vector.tensor_tensor(col(30, 5), col(30, 5), weight, ALU.mult))
                link(nc.vector.tensor_tensor(col(35, 5), mean, weight, ALU.mult))
                link(nc.vector.tensor_reduce(col(14), col(35, 5), AX.X, ALU.add))
                link(nc.vector.tensor_reduce(col(15), col(30, 5), AX.X, ALU.add))
                link(nc.vector.tensor_scalar(col(16), consts[:, K_LOWER:K_LOWER + 1], 1.0, col(21), ALU.add, ALU.mult))
                link(nc.vector.tensor_tensor(col(17), col(12), col(22), ALU.mult))
                link(nc.vector.tensor_tensor(col(18), col(16), col(17), ALU.add))
                link(nc.vector.tensor_tensor(col(0), col(14), col(18), ALU.add))
                link(nc.vector.scalar_tensor_tensor(out=col(18), in0=col(17), scalar=2.0, in1=col(16),
                                                    op0=ALU.mult, op1=ALU.add))
                link(nc.vector.tensor_tensor(col(18), col(18), col(21), ALU.mult))
                link(nc.vector.scalar_tensor_tensor(out=col(19), in0=col(13), scalar=col(22), in1=col(22),
                                                    op0=ALU.mult, op1=ALU.mult))
                link(nc.vector.tensor_tensor(col(18), col(18), col(19), ALU.add))
                nc.vector.tensor_tensor(col(1), col(15), col(18), ALU.add).then_inc(partial_ready, 1)
                total(i * 2 + 2, col(7), col(25), col(26))
                sc = scal[:, bass.ds(i, 1), :].rearrange("p o k -> p (o k)")
                link(nc.vector.tensor_tensor(sc[:, 0:1], col(25), col(22), ALU.mult))
                link(nc.vector.tensor_tensor(col(8), col(21), col(7), ALU.subtract))
                link(nc.vector.tensor_tensor(sc[:, 1:2], col(8), col(25), ALU.mult))
                link(nc.vector.tensor_copy(sc[:, 2:3], col(25)))
                link(nc.vector.scalar_tensor_tensor(out=sc[:, 3:4], in0=col(7), scalar=-1.0, in1=col(25),
                                                    op0=ALU.mult, op1=ALU.mult))
                nc.vector.tensor_tensor(sc[:, 4:5], col(7), biases[:], ALU.add).then_inc(scal_ready, 1)
                v.wait_ge(centre_ready, i + 1)
                nc.vector.scalar_tensor_tensor(out=w_sum[:], in0=eyes[:], scalar=col(26), in1=w_centre[:],
                                               op0=ALU.mult, op1=ALU.add).then_inc(w_sum_ready, 1)
                assert steps[1] == STEPS_IMAGE, steps

        @block.scalar
        def _(act):
            def load(i, g, t, s, upper):
                src = x[i].rearrange("c (b r) w -> c r b w", r=Q)
                ysrc = y_quarter[i].rearrange("c (b r) w -> c r b w", r=Q)
                rows = bass.ds(g * GROUP, GROUP)
                for r in range(Q):
                    if upper:
                        act.dma_start(raw[r:P:Q, s, :, 0:WQ], ysrc[:, r, rows, :]
                                      ).then_inc(raw_in[s], 16)
                        act.dma_start(raw[r:P:Q, s, :, WQ:W], src[:, r, rows, WQ:W]
                                      ).then_inc(raw_in[s], 16)
                    else:
                        act.dma_start(raw[r:P:Q, s, :, :], src[:, r, rows, :]
                                      ).then_inc(raw_in[s], 32)

            def take_norm(i):
                nc.scalar.copy(norm_now[:], scal[:, bass.ds(i, 1), 0:4].rearrange("p o k -> p (o k)")
                               ).then_inc(norm_now_ready, 1)

            def take_shift(i, s):
                nc.scalar.copy(shift_now[:, s:s + 1], scal[:, bass.ds(i, 1), 4:5].rearrange("p o k -> p (o k)")
                               ).then_inc(shift_now_ready, 1)

            def prepare(i, t, n, s, upper):
                act.wait_ge(norm_now_ready, i + 1)
                act.wait_ge(raw_in[s], n * (32 * Q) + 32 * Q)
                if upper:
                    nc.scalar.activation(raw[:, s, :, 0:WQ], raw[:, s, :, 0:WQ], ACT.Identity,
                                         bias=norm_now[:, 3:4], scale=norm_now[:, 2:3])
                    nc.scalar.activation(raw[:, s, :, WQ:W], raw[:, s, :, WQ:W], ACT.Identity,
                                         bias=norm_now[:, 1:2], scale=norm_now[:, 0:1]).then_inc(normed, 1)
                else:
                    nc.scalar.activation(raw[:, s, :, :], raw[:, s, :, :], ACT.Identity,
                                         bias=norm_now[:, 1:2], scale=norm_now[:, 0:1]).then_inc(normed, 1)
                act.wait_ge(normed, t + 1)

            def high_part(s):
                nc.scalar.copy(high[:, GROUP * s:GROUP * s + GROUP, 1:W + 1], raw[:, s, :, :]
                               ).then_inc(high_ready, 1)

            ABOVE = {0: ((0, 1, 2 * GROUP - 1), (1, GROUP - 1, 0)), 1: ((0, GROUP, GROUP - 1),)}
            BELOW = {0: ((0, GROUP, 1),), 1: ((0, GROUP - 1, GROUP + 1), (GROUP - 1, 1, 0))}

            def copy_halo(pieces, row, first, s, done, edge):
                for at, n, src in pieces:
                    for part, tile in ((first, high), (first + 2, low)):
                        dst = halo[C * part:C * part + C, s, at:at + n, :].bitcast(F32)
                        if edge and n == 1:
                            act.dma_start(dst, zeros[:].bitcast(F32).rearrange("p (o w) -> p o w", o=1)
                                          ).then_inc(done, 32 // len(pieces))
                        else:
                            act.dma_start(dst, tile[row:P:Q, src:src + n, :].bitcast(F32)
                                          ).then_inc(done, 32 // len(pieces))

            def above(s, edge=False):
                copy_halo(ABOVE[s], Q - 1, 0, s, above_in[s], edge)

            def below(s, edge=False):
                copy_halo(BELOW[s], 0, 1, s, below_in[s], edge)

            def step(i, g, t, n, s, load_next=None, prepare_next=None, last=False, first_next=False):
                if prepare_next is not None or load_next is not None or not last:
                    act.wait_ge(low_ready, t + 2)
                act.wait_ge(sums_read[s], n + 1)
                below(s, edge=last)
                take_shift(i, s)
                if not (last and prepare_next is None):
                    above(1 - s, edge=last)
                if load_next is not None:
                    load_next()
                if prepare_next is not None:
                    prepare_next()
                    act.wait_ge(main_done, t + 1)
                    act.wait_ge(below_in[s], n * 64 + 64)
                    act.wait_ge(above_in[1 - s], (n + (1 if s == 0 else 2)) * 64)
                    high_part(s)
                act.wait_ge(sums_ready, t + 1)
                act.wait_ge(out_stored[s], n * (16 * Q) + 16)
                act.wait_ge(shift_now_ready, t + 1)
                nc.scalar.activation(outs[:, s, :, :], sums[:, s, :, :], ACT.Identity,
                                     bias=shift_now[:, s:s + 1]).then_inc(sums_read[s], 1)

            def start_image(i):
                act.wait_ge(y_stored, i * (16 * Q) + 16 * (Q + 1))

            act.wait_ge(conv_zeroed, 1)
            start_image(0)
            load(0, 0, 0, 0, True)
            load(0, 1, 1, 1, True)
            act.wait_ge(scal_ready, 1)
            take_norm(0)
            for s in range(2):
                prepare(0, s, 0, s, True)
                high_part(s)
            act.wait_ge(low_ready, 1)
            above(0, edge=True)
            load(0, 2, 2, 0, True)

            def image(i, more):
                t0, n0 = i * G, i * (G // 2)

                def pair(g, load_upper, prepare_upper):
                    for s in range(2):
                        step(i, g + s, t0 + g + s, n0 + g_half(g), s,
                             load_next=lambda: load(i, g + (s + 3), None, 1 - s, load_upper[s]),
                             prepare_next=lambda: prepare(i, t0 + g + (s + 2), n0 + g_half(g) + 1, s,
                                                          prepare_upper))

                def g_half(g):
                    return halves[0]

                halves = [None]
                with act.Fori(0, GQ // 2 - 2) as k:
                    halves[0] = k
                    pair(k * 2, (True, True), True)
                halves[0] = GQ // 2 - 2
                pair(GQ - 4, (True, False), True)
                with act.Fori(GQ // 2 - 1, G // 2 - 2) as k:
                    halves[0] = k
                    pair(k * 2, (False, False), False)
                for g in range(G - 4, G):
                    s = g % 2
                    t, n = t0 + g, n0 + g // 2
                    if g + 3 < G:
                        load_next = lambda: load(i, g + 3, None, 1 - s, False)
                    elif more:
                        def load_next():
                            if g + 3 == G:
                                start_image(i + 1)
                            if g + 2 == G:
                                act.wait_ge(scal_ready, i + 2)
                            load(i + 1, g + 3 - G, None, 1 - s, True)
                            if g + 2 == G:
                                take_norm(i + 1)
                    else:
                        load_next = None
                    if g + 2 < G:
                        prepare_next = lambda: prepare(i, t + 2, n + 1, s, False)
                    elif more:
                        def prepare_next():
                            prepare(i + 1, t + 2, n + 1, s, True)
                    else:
                        prepare_next = None
                    step(i, g, t, n, s, load_next, prepare_next, last=g == G - 1)

            if B > 1:
                with act.Fori(0, B - 1) as i:
                    image(i, True)
            image(B - 1, False)

        @block.gpsimd
        def _(pool):
            for s in range(2):
                pool.dma_start(spare[:, 2 + s:3 + s], bias.rearrange("(c o) -> c o", o=1)
                               ).then_inc(out_stored[s], 16)
            nc.gpsimd.memset(high[:].bitcast(F32), 0.0).then_inc(sums_read[0], 1)
            nc.gpsimd.memset(low[:].bitcast(F32), 0.0).then_inc(sums_read[1], 1)
            nc.gpsimd.memset(halo[:].bitcast(F32), 0.0).then_inc(centre_ready, 1)
            nc.gpsimd.memset(zeros[:].bitcast(F32), 0.0).then_inc(conv_zeroed, 1)

            def low_part(t, s):
                pool.wait_ge(high_ready, t + 1)
                blocks = slice(GROUP * s, GROUP * s + GROUP)
                nc.gpsimd.tensor_tensor(low[:, blocks, 1:W + 1], raw[:, s, :, :],
                                        high[:, blocks, 1:W + 1].bitcast(F32), ALU.subtract
                                        ).then_inc(low_ready, 1)

            def centre(i):
                nc.gpsimd.tensor_copy(w_high[:, 1, :], w_sum[:]).then_inc(centre_high_ready, 1)
                pool.wait_ge(centre_high_ready, i + 1)
                nc.gpsimd.tensor_tensor(w_low[:, 1, :], w_sum[:], w_high[:, 1, :].bitcast(F32),
                                        ALU.subtract).then_inc(centre_ready, 1)

            def store(i, g, n, s):
                pool.wait_ge(sums_read[s], n + 2)
                for r in range(Q):
                    pool.dma_start(out[i].rearrange("c (b r) w -> c r b w", r=Q)
                                   [:, r, bass.ds(g * GROUP, GROUP), :],
                                   outs[r:P:Q, s, :, :]).then_inc(out_stored[s], 16)

            low_part(0, 0)
            pool.wait_ge(w_sum_ready, 1)
            low_part(1, 1)
            centre(0)

            def image(i, more):
                t0, n0 = i * G, i * (G // 2)
                with pool.Fori(0, G // 2 - 1) as k:
                    for s in range(2):
                        low_part(t0 + k * 2 + (s + 2), s)
                        store(i, k * 2 + s, n0 + k, s)
                for s in range(2):
                    if more:
                        if s == 1:
                            pool.wait_ge(w_sum_ready, i + 2)
                        low_part(t0 + (G + s), s)
                        if s == 1:
                            centre(i + 1)
                    store(i, G - 2 + s, n0 + (G // 2 - 1), s)

            if B > 1:
                with pool.Fori(0, B - 1) as i:
                    image(i, True)
            image(B - 1, False)
            for s in range(2):
                pool.wait_ge(out_stored[s], 16 * Q * B * G // 2 + 16)

        @block.tensor
        def _(pe):
            def sum_partitions(n):
                pe.wait_ge(partial_ready, n + 1)
                nc.tensor.matmul(sums[:, 0, 0, 0:2], groups[:], small[:, 0:2], start=True,
                                 stop=True).then_inc(total_ready, 1)

            def group(i, t, n, s, totals):
                if s == 0:
                    pe.wait_ge(total_read, totals)
                pe.wait_ge(low_ready, t + 1)
                pe.wait_ge(sums_read[s], n + 1)
                for k, (kx, weights, parts) in enumerate(
                        (kx, wgt, prt) for kx in (0, 2, 1)
                        for wgt, prt in ((w_high, high), (w_low, high), (w_high, low))):
                    if kx == 1:
                        pe.wait_ge(centre_ready, i + 2)
                    for j in range(GROUP):
                        mm = nc.tensor.matmul(sums[:, s, j, :], weights[:, kx, :],
                                              parts[:, GROUP * s + j, kx:kx + W],
                                              start=k == 0, stop=False)
                mm.then_inc(main_done, 1)
                pe.wait_ge(above_in[s], n * 64 + 64)
                pe.wait_ge(below_in[s], n * 64 + 64)
                for kx in range(3):
                    for weights in (wt_high, wt_low):
                        for j in range(GROUP):
                            mm = nc.tensor.matmul(sums[:, s, j, :], weights[:, kx, :],
                                                  halo[:, s, j, kx:kx + W], start=False,
                                                  stop=kx == 2 and weights is wt_low)
                mm.then_inc(sums_ready, 1)

            def image(i, more):
                t0, n0 = i * G, i * (G // 2)
                with pe.Fori(0, XSTAT_AT // 2) as k:
                    for s in range(2):
                        group(i, t0 + k * 2 + s, n0 + k, s, i * 2 + 2)
                if more:
                    pe.wait_ge(sums_read[0], n0 + (XSTAT_AT // 2 + 1))
                    sum_partitions(i * 2 + 2)
                with pe.Fori(XSTAT_AT // 2, YSTAT_AT // 2) as k:
                    for s in range(2):
                        group(i, t0 + k * 2 + s, n0 + k, s, i * 2 + (3 if more else 2))
                if more:
                    pe.wait_ge(sums_read[0], n0 + (YSTAT_AT // 2 + 1))
                    sum_partitions(i * 2 + 3)
                with pe.Fori(YSTAT_AT // 2, G // 2) as k:
                    for s in range(2):
                        group(i, t0 + k * 2 + s, n0 + k, s, i * 2 + (4 if more else 2))

            pe.wait_ge(consts_in, 16 * (3 + Q))
            sum_partitions(0)
            pe.wait_ge(total_read, 1)
            sum_partitions(1)
            pe.wait_ge(total_read, 2)
            if B > 1:
                with pe.Fori(0, B - 1) as i:
                    image(i, True)
            image(B - 1, False)


STEPS_CHUNKS = 8
STEPS_IMAGE = 287


def shape_constants(H):
    q = np.arange(P) % Q
    lower = (q >= 2).astype(np.float32)
    cols = [lower, (q > 0).astype(np.float32)]
    cols += [np.full(P, 1 / 4) * lower, np.full(P, 1 / 4), np.full(P, 1 / 16) * lower,
             np.full(P, 1 / 16), np.full(P, 1 / 32)]
    for l in range(LEVELS):
        for r in range(H // Q >> (l + 1)):
            cols.append(np.where((q == 0) & (r == 0), E0[l] * E0[l], E0[l]) - 1.0)
    return np.stack([*cols, (q == 0).astype(np.float32)], 1).astype(np.float32)


def kernel(x, L1_conv_weight, L1_conv_bias):
    import concourse.bacc as _bacc
    from concourse.bass_utils import run_bass_kernel_spmd as _run

    x = np.ascontiguousarray(x)
    p = np.arange(P)
    arrays = {
        "x": x,
        "w_taps": np.ascontiguousarray(np.transpose(L1_conv_weight, (1, 2, 3, 0))),
        "bias": np.ascontiguousarray(L1_conv_bias),
        "same_group": (p[:, None] // (2 * Q) == p[None, :] // (2 * Q)).astype(np.float32),
        "eye": np.eye(P, dtype=np.float32),
        "shape_consts": shape_constants(x.shape[2]),
    }
    nc = _bacc.Bacc("TRN2", target_bir_lowering=False, num_devices=1)
    args = [nc.dram_tensor(n, a.shape, mybir.dt.from_np(a.dtype), kind="ExternalInput").ap()
            for n, a in arrays.items()]
    args.append(nc.dram_tensor("out", x.shape, F32, kind="ExternalOutput").ap())
    group_norm_pyramid_conv(nc, *args)
    r = _run(nc, [arrays], core_ids=[0])
    return r.results[0]["out"]
```

```python
from contextlib import ExitStack

import numpy as np

import concourse.bass as bass
from concourse import mybir

ALU = mybir.AluOpType
ACT = mybir.ActivationFunctionType
AX = mybir.AxisListType
F32 = mybir.dt.float32
F32R = mybir.dt.float32r
I32 = mybir.dt.int32

P = 128
Q = 4
EPS = 1e-5
PAD = 2
GROUP = 4
LEVELS = 3
E0 = (0.75, 0.625, 0.5625)
RSQRT_SEED = 0x5F3759DF
NEWTON_STEPS = 4
CHUNK = 4
MCHUNK = 8
K_LOWER, K_TOP, K_REGION, K_EDGE = 0, 1, 2, 7


def group_norm_pyramid_conv(nc, x, w_taps, bias, same_group, eye, shape_consts, out):
    B, C, H, W = x.shape
    assert C * Q == P and H == W and w_taps.shape[0] == C
    HW4 = H // Q
    N1 = HW4 // CHUNK
    WQ = W // 2
    LR = [HW4 >> (l + 1) for l in range(LEVELS)]
    LW = [W >> (l + 1) for l in range(LEVELS)]
    N2 = [r // MCHUNK for r in LR]
    NM = sum(N2)
    NA = N1 + NM
    assert NA % 2 == 0 and all(n % 2 == 0 for n in N2) and N1 % 2 == 0
    GR = GROUP * Q
    G = H // GR
    GQ = G // 2
    WP = W + 2
    GN = float(2 * H * W)
    UNIT = float(HW4 * WQ)
    SLOT = CHUNK * (W + 2 * PAD)
    STORE1 = 16 * (1 + Q // 2)
    LAG = 3
    XSTAT_AT, YSTAT_AT = G - 14, G - 4

    y_quarter = nc.dram_tensor("y_quarter", (B, C, H // 2, WQ), F32, kind="Internal").ap()

    with ExitStack() as ctx:
        def sb(name, shape, dt=F32):
            return ctx.enter_context(nc.sbuf_tensor(name, shape, dt))

        def sem(name):
            return ctx.enter_context(nc.semaphore(name))

        xa = sb("xa", [P, 2, SLOT])
        xlast = sb("xlast", [P, W + PAD])
        hblur = sb("hblur", [P, 5 * WQ])
        level = [sb(f"level{l}", [P, LR[l], LW[l] + PAD]) for l in range(LEVELS)]
        xstats = sb("xstats", [P, 2, N1 * 2, 6])
        ystats = [sb(f"ystats{k}", [P, n, 6]) for k, n in enumerate((16, 16, 4, 4, 2))]
        moments = sb("moments", [P, 7, 2])
        small = sb("small", [P, 64])
        consts = sb("consts", [P, shape_consts.shape[1]])
        groups = sb("groups", [P, P])
        eyes = sb("eyes", [P, P])
        scal = sb("scal", [P, B, 8])
        norm_now = sb("norm_now", [P, 4])
        shift_now = sb("shift_now", [P, 2])
        raw = sb("raw", [P, 2, GROUP, W])
        parts = sb("parts", [P, 2, 2 * GROUP, WP], F32R)
        halo = sb("halo", [P, 2, GROUP, WP], F32R)
        zeros = sb("zeros", [2 * C, WP], F32R)
        outs = sb("outs", [P, 2, GROUP, W])
        w_high = sb("w_high", [P, 3, P], F32R)
        w_low = sb("w_low", [P, 3, P], F32R)
        wt_high = sb("wt_high", [P, 3, P], F32R)
        wt_low = sb("wt_low", [P, 3, P], F32R)
        w_centre = sb("w_centre", [P, P])
        biases = sb("biases", [P, 1])
        spare = sb("spare", [C, 4])
        w_sum = sb("w_sum", [P, P])
        sums = ctx.enter_context(nc.psum_tensor("sums", [P, 2, GROUP, W], F32))

        consts_in = sem("consts_in")
        weights_zeroed = sem("weights_zeroed")
        weights_in = sem("weights_in")
        weights_split = sem("weights_split")
        pads_zeroed = sem("pads_zeroed")
        conv_zeroed = sem("conv_zeroed")
        xa_in = [sem(f"xa_in{s}") for s in range(2)]
        xa_free = [sem(f"xa_free{s}") for s in range(2)]
        xlast_in = sem("xlast_in")
        xlast_free = sem("xlast_free")
        dve = sem("dve")
        y1_ready = sem("y1_ready")
        y23_ready = sem("y23_ready")
        y1_stored = sem("y1_stored")
        y2_stored = sem("y2_stored")
        y_stored = sem("y_stored")
        partial_ready = sem("partial_ready")
        total_ready = sem("total_ready")
        total_read = sem("total_read")
        scal_ready = sem("scal_ready")
        w_sum_ready = sem("w_sum_ready")
        centre_high_ready = sem("centre_high_ready")
        centre_ready = sem("centre_ready")
        raw_in = [sem(f"raw_in{s}") for s in range(2)]
        raw3_in = [sem(f"raw3_in{s}") for s in range(2)]
        norm_now_ready = sem("norm_now_ready")
        shift_now_ready = sem("shift_now_ready")
        normed = sem("normed")
        high_ready = sem("high_ready")
        low_ready = sem("low_ready")
        above_in = [sem(f"above_in{s}") for s in range(2)]
        below_in = [sem(f"below_in{s}") for s in range(2)]
        main_done = sem("main_done")
        sums_ready = sem("sums_ready")
        sums_read = [sem(f"sums_read{s}") for s in range(2)]
        out_stored = [sem(f"out_stored{s}") for s in range(2)]

        high, low = parts[:, 0], parts[:, 1]

        wm = [level[0][:, 3 * k:3 * k + 3, 0:P] for k in range(2)]
        LEFT, RIGHT = slice(PAD, PAD + WQ), slice(PAD + WQ, PAD + W)

        def x_rows(slot):
            return xa[:, slot, :].rearrange("p (r w) -> p r w", r=CHUNK)

        def m_rows(slot, width):
            return xa[:, slot, :].rearrange("p (r w) -> p r w", r=MCHUNK)[:, :, PAD:PAD + width]

        def store_y1(sp, i, k):
            rows = slice(MCHUNK * k, MCHUNK * k + MCHUNK)
            half = LW[1]
            sp.wait_ge(y1_ready, i * N2[0] + (k + 1))
            sp.dma_start(y_quarter[i].rearrange("c (q r) w -> (c q) r w", q=Q)[:, rows, half:],
                         level[0][:, rows, PAD + half:PAD + WQ]).then_inc(y1_stored, 16)
            for q in range(Q // 2, Q):
                sp.dma_start(y_quarter[i].rearrange("c (q r) w -> c q r w", q=Q)[:, q, rows, 0:half],
                             level[0][q:P:Q, rows, PAD:PAD + half]).then_inc(y1_stored, 16)

        def store_level(sp, i, l, done):
            for q in reversed(range(Q)):
                sp.dma_start(y_quarter[i, :, q * LR[l]:(q + 1) * LR[l], 0:LW[l]],
                             level[l][q:P:Q, :, PAD:PAD + LW[l]]).then_inc(done, 16)

        block = ctx.enter_context(nc.Block())

        @block.sync
        def _(sp):
            for k, done in enumerate((y1_stored, y_stored)):
                sp.dma_start(spare[:, k:k + 1], bias.rearrange("(c o) -> c o", o=1)).then_inc(done, 16)
            sp.dma_start(consts[:], shape_consts).then_inc(consts_in, 16)
            sp.dma_start(groups[:], same_group).then_inc(consts_in, 16)
            sp.dma_start(eyes[:], eye).then_inc(consts_in, 16)
            for r in range(Q):
                sp.dma_start(biases[r:P:Q, :], bias.rearrange("(c o) -> c o", o=1)).then_inc(consts_in, 16)
            sp.wait_ge(weights_zeroed, 1)
            for r in range(Q):
                for o in range(Q):
                    if 0 <= r - o + 1 < 3:
                        sp.dma_start(wm[0][r:P:Q, :, C * o:C * o + C],
                                     w_taps[:, r - o + 1]).then_inc(weights_in, 16)
            for part in range(2):
                for first, ky, o in ((0, 0, 0), (2 * C, 2, Q - 1)):
                    sp.dma_start(wm[1][first + part:first + 2 * C:2, :, C * o:C * o + C],
                                 w_taps[:, ky]).then_inc(weights_in, 16)

            with sp.Fori(0, B) as i:
                rows = x[i].rearrange("c (q r) w -> (c q) r w", q=Q)
                chunks = x[i].rearrange("c (q k s r) w -> (c q) k s r w", q=Q, s=2, r=CHUNK)
                sp.wait_ge(xlast_free, i + 1)
                sp.dma_start(xlast[:, PAD:PAD + W], rows[:, HW4 - 1, :]).then_inc(xlast_in, 16)
                with sp.Fori(0, N1 // 2) as k:
                    for s in range(2):
                        sp.wait_ge(xa_free[s], i * (NA // 2) + k + 1)
                        sp.dma_start(x_rows(s)[:, :, PAD:PAD + W],
                                     chunks[:, bass.ds(k, 1), s].rearrange("p o r w -> p (o r) w")
                                     ).then_inc(xa_in[s], 16 * Q)
                done = N1
                for l in range(LEVELS):
                    part = x[i, :, 0:H >> (l + 1), 0:LW[l]].rearrange("c (q r) w -> c q r w", q=Q)
                    for k in range(N2[l]):
                        s = k % 2
                        sp.wait_ge(xa_free[s], i * (NA // 2) + (done // 2 + k // 2 + 1))
                        for q in reversed(range(Q)):
                            left = LW[1] if l == 0 and q < Q // 2 else 0
                            sp.dma_start(m_rows(s, LW[l])[q:P:Q, :, left:],
                                         part[:, q, MCHUNK * k:MCHUNK * k + MCHUNK, left:]
                                         ).then_inc(xa_in[s], 16)
                        if l == 0 and k >= 2:
                            store_y1(sp, i, k - 2)
                    if l == 0:
                        store_y1(sp, i, N2[0] - 2)
                        store_y1(sp, i, N2[0] - 1)
                    done += N2[l]
                sp.wait_ge(y1_stored, i * (STORE1 * N2[0]) + (STORE1 * N2[0] + 16))
                sp.wait_ge(y23_ready, i * 2 + 1)
                store_level(sp, i, 1, y2_stored)
                sp.wait_ge(y23_ready, i * 2 + 2)
                sp.wait_ge(y2_stored, i * (16 * Q) + 16 * Q)
                store_level(sp, i, 2, y_stored)
            sp.wait_ge(y_stored, 16 * Q * B + 16)

        @block.vector
        def _(v):
            steps = [0, 0]

            def link(ins):
                steps[1] += 1
                ins.then_inc(dve, 1)
                v.wait_ge(dve, steps[0] + steps[1])

            one, even = shape_consts.shape[1] - 2, shape_consts.shape[1] - 1

            def col(n, width=1):
                return small[:, n:n + width]

            def carry_wait():
                nc.vector.memset(col(63), 0.0)

            def blur(src, n, width, dst, between=lambda k: None):
                def link(ins, k):
                    steps[1] += 1
                    ins.then_inc(dve, 1)
                    between(k)
                    v.wait_ge(dve, steps[0] + steps[1])

                h = hblur[:, 0:(n + 1) * width].rearrange("p (r w) -> p r w", w=width)
                left, mid = src[:, :, 1:1 + 2 * width:2], src[:, :, 2:2 + 2 * width:2]
                right = src[:, :, 3:2 + 2 * width:2]
                link(nc.vector.tensor_tensor(h[:, 1:n + 1, :], left, right, ALU.add), 0)
                link(nc.vector.scalar_tensor_tensor(out=h[:, 1:n + 1, :], in0=mid, scalar=2.0,
                                                    in1=h[:, 1:n + 1, :], op0=ALU.mult, op1=ALU.add), 1)
                link(nc.vector.tensor_tensor(dst, h[:, 0:n - 1:2, :], h[:, 2:n + 1:2, :], ALU.add), 2)
                nc.vector.scalar_tensor_tensor(out=dst, in0=h[:, 1:n:2, :], scalar=2.0, in1=dst,
                                               op0=ALU.mult, op1=ALU.add)
                link(nc.vector.tensor_copy(h[:, 0, :], h[:, n, :]), 3)

            def blur_last_row(src, width):
                shift = [max(p - 1, 0) for p in range(32)]
                carry_wait()
                link(nc.vector.stream_shuffle(src, src, shift))
                h = hblur[:, 0:width]
                link(nc.vector.tensor_tensor(h, src[:, 1:1 + 2 * width:2], src[:, 3:2 + 2 * width:2], ALU.add))
                link(nc.vector.scalar_tensor_tensor(out=h, in0=src[:, 2:2 + 2 * width:2], scalar=2.0,
                                                    in1=h, op0=ALU.mult, op1=ALU.add))
                link(nc.vector.tensor_scalar(h, h, consts[:, K_TOP:K_TOP + 1], None, ALU.mult))

            def rsqrt(dst, var, t0, t1):
                link(nc.vector.tensor_scalar(t0.bitcast(I32), var.bitcast(I32), 1, None,
                                             ALU.arith_shift_right))
                link(nc.vector.tensor_scalar(dst.bitcast(I32), t0.bitcast(I32), -1.0,
                                             float(RSQRT_SEED), ALU.mult, ALU.add))
                for _ in range(NEWTON_STEPS):
                    link(nc.vector.scalar_tensor_tensor(out=t0, in0=dst, scalar=dst, in1=var,
                                                        op0=ALU.mult, op1=ALU.mult))
                    link(nc.vector.tensor_scalar(t1, t0, -0.5, 1.5, ALU.mult, ALU.add))
                    link(nc.vector.tensor_tensor(dst, dst, t1, ALU.mult))


            def total(n_done, mean, r, sigma):
                v.wait_ge(total_ready, n_done)
                nc.vector.tensor_scalar(col(2, 2), sums[:, 0, 0, 0:2], UNIT / GN, None,
                                        ALU.mult).then_inc(total_read, 1)
                v.wait_ge(total_read, n_done)
                link(nc.vector.tensor_copy(mean, col(2)))
                link(nc.vector.tensor_tensor(col(4), col(2), col(2), ALU.mult))
                link(nc.vector.tensor_tensor(col(4), col(3), col(4), ALU.subtract))
                link(nc.vector.tensor_scalar(col(4), col(4), 0.0, EPS, ALU.max, ALU.add))
                rsqrt(r, col(4), col(5), col(6))
                link(nc.vector.tensor_tensor(sigma, col(4), r, ALU.mult))

            nc.vector.memset(xlast[:], 0.0)
            for l in range(1, LEVELS):
                nc.vector.memset(level[l][:], 0.0)
            nc.vector.memset(xa[:], 0.0)
            nc.vector.memset(level[0][:], 0.0).then_inc(weights_zeroed, 1)
            v.wait_ge(weights_zeroed, 1)
            v.wait_ge(weights_in, 16 * 14)
            v.wait_ge(consts_in, 16 * (3 + Q))
            for fine, hi, lo in ((wm[0], w_high, w_low), (wm[1], wt_high, wt_low)):
                for kx in range(3):
                    f = fine[:, kx, :].rearrange("p (o c) -> p c o", o=Q)
                    h = hi[:, kx, :].rearrange("p (c o) -> p c o", o=Q)
                    l = lo[:, kx, :].rearrange("p (c o) -> p c o", o=Q)
                    link(nc.vector.tensor_copy(h, f))
                    link(nc.vector.tensor_tensor(l, f, h.bitcast(F32), ALU.subtract))
            link(nc.vector.tensor_scalar(wt_low[:], wt_low[:].bitcast(F32),
                                       consts[:, even:even + 1], None, ALU.mult))
            link(nc.vector.tensor_copy(w_centre[:].rearrange("p (c o) -> p c o", o=Q),
                                       wm[0][:, 1, :].rearrange("p (o c) -> p c o", o=Q)))
            nc.vector.memset(level[0][:, 0:6, 0:PAD], 0.0).then_inc(weights_split, 1)
            v.wait_ge(weights_split, 1)
            nc.vector.memset(small[:, 0:16], 0.0).then_inc(xa_free[0], 1)
            nc.vector.memset(small[:, 16:32], 0.0).then_inc(xa_free[1], 1)
            nc.vector.memset(small[:, 32:64], 0.0).then_inc(xlast_free, 1)
            for s in range(2):
                v.wait_ge(xa_free[s], 1)
            v.wait_ge(xlast_free, 1)

            first = steps[1]
            with v.Fori(0, B) as i:
                base = i * STEPS_IMAGE + first
                steps[0], steps[1] = base, 0
                v.wait_ge(y1_stored, i * (STORE1 * N2[0]) + 16)
                v.wait_ge(y_stored, i * (16 * Q) + 16)
                v.wait_ge(xlast_in, i * 16 + 16)
                blur_last_row(xlast[:, 0:PAD + W], WQ)
                before = steps[1]
                carry_wait()
                with v.Fori(0, N1 // 2) as k:
                    steps[0], steps[1] = base + k * STEPS_CHUNKS + before, 0
                    for s in range(2):
                        v.wait_ge(xa_in[s], i * (8 * NA * Q) + k * (16 * Q) + 16 * Q)

                        def stats(n):
                            half, pair = divmod(n, CHUNK // 2)
                            ins = nc.vector.bn_stats(
                                xstats[:, half, bass.ds(k * CHUNK + (s * CHUNK // 2 + pair), 1), :]
                                .rearrange("p o k -> p (o k)"),
                                x_rows(s)[:, 2 * pair:2 * pair + 2, (LEFT, RIGHT)[half]])
                            if n == CHUNK - 1:
                                ins.then_inc(xa_free[s], 1)

                        blur(x_rows(s), CHUNK, WQ,
                             level[0][:, bass.ds(k * CHUNK + s * CHUNK // 2, CHUNK // 2), PAD:PAD + WQ],
                             between=stats)
                    assert steps[1] == STEPS_CHUNKS, steps
                steps[0], steps[1] = base, before + STEPS_CHUNKS * (N1 // 2)
                v.wait_ge(xa_free[1], i * (NA // 2) + (N1 // 2 + 1))
                carry_wait()
                nc.vector.bn_aggr(moments[:, 0, :], xstats[:, 0, :, :])
                link(nc.vector.bn_aggr(moments[:, 1, :], xstats[:, 1, :, :]))
                mean, var = moments[:, 0:2, 0], moments[:, 0:2, 1]
                link(nc.vector.tensor_tensor(col(10, 2), mean, mean, ALU.mult))
                link(nc.vector.tensor_tensor(col(10, 2), col(10, 2), var, ALU.add))
                link(nc.vector.tensor_tensor(col(0), moments[:, 0, 0:1], moments[:, 1, 0:1], ALU.add))
                nc.vector.tensor_tensor(col(1), col(10), col(11), ALU.add).then_inc(partial_ready, 1)
                link(nc.vector.scalar_tensor_tensor(out=col(12), in0=moments[:, 0, 0:1],
                                                    scalar=consts[:, K_LOWER:K_LOWER + 1],
                                                    in1=moments[:, 1, 0:1], op0=ALU.mult, op1=ALU.add))
                link(nc.vector.scalar_tensor_tensor(out=col(13), in0=col(10),
                                                    scalar=consts[:, K_LOWER:K_LOWER + 1],
                                                    in1=col(11), op0=ALU.mult, op1=ALU.add))
                def blur_start(l):
                    last = xlast[:, 0:PAD + LW[l - 1]]
                    link(nc.vector.tensor_copy(last[:, PAD:], level[l - 1][:, LR[l - 1] - 1, PAD:]))
                    blur_last_row(last, LW[l])

                def blur_level(l, k):
                    blur(level[l - 1][:, MCHUNK * k:MCHUNK * k + MCHUNK, :], MCHUNK, LW[l],
                         level[l][:, MCHUNK // 2 * k:MCHUNK // 2 * (k + 1), PAD:])

                def y_start(l):
                    link(nc.vector.tensor_scalar(col(23), col(20), 16.0 ** -(l + 1), None, ALU.mult))
                    link(nc.vector.tensor_scalar(col(24), col(21), E0[l] - 1.0, None, ALU.mult))
                    link(nc.vector.tensor_tensor(col(24), col(24), consts[:, one:one + 1], ALU.mult))

                def y_level(l, k):
                    seen = (N1 + sum(N2[:l])) // 2 + k // 2
                    edge = K_EDGE + sum(LR[:l]) + MCHUNK * k
                    s = k % 2
                    y = level[l][:, MCHUNK * k:MCHUNK * k + MCHUNK, PAD:]
                    v.wait_ge(xa_in[s], i * (8 * NA * Q) + 16 * Q * (seen + 1))
                    link(nc.vector.scalar_tensor_tensor(out=y, in0=y, scalar=col(23),
                                                        in1=m_rows(s, LW[l]),
                                                        op0=ALU.mult, op1=ALU.add))
                    nc.vector.tensor_scalar(y, y, col(21), None, ALU.add).then_inc(xa_free[s], 1)
                    v.wait_ge(xa_free[s], i * (NA // 2) + (seen + 2))
                    ec = consts[:, edge:edge + MCHUNK].rearrange("p (r o) -> p r o", o=1)
                    last = nc.vector.scalar_tensor_tensor(out=y[:, :, 0:1], in0=ec, scalar=col(21),
                                                          in1=y[:, :, 0:1], op0=ALU.mult, op1=ALU.add)
                    if k == 0:
                        link(last)
                        last = nc.vector.tensor_scalar(y[:, 0, 1:], y[:, 0, 1:], col(24), None, ALU.add)
                    if l == 0:
                        last.then_inc(y1_ready, 1)
                        v.wait_ge(y1_ready, i * N2[0] + (k + 1))
                    else:
                        link(last)
                    if l < LEVELS - 1:
                        n = 512 // (LW[l] // 2)
                        for j in range(MCHUNK // n):
                            for half in range(2):
                                last = nc.vector.bn_stats(
                                    ystats[2 * l + half][:, k * (MCHUNK // n) + j, :],
                                    y[:, n * j:n * j + n, half * LW[l] // 2:(half + 1) * LW[l] // 2])
                    else:
                        last = nc.vector.bn_stats(ystats[2 * l][:, k, :], y)
                    if l and k == N2[l] - 1:
                        last.then_inc(y23_ready, 1)

                blur_start(1)
                for k in range(N2[0] + LAG):
                    if k == LAG:
                        total(i * 2 + 1, col(7), col(20), col(8))
                        link(nc.vector.scalar_tensor_tensor(out=col(21), in0=col(7), scalar=-1.0,
                                                            in1=col(20), op0=ALU.mult, op1=ALU.mult))
                        link(nc.vector.tensor_scalar(col(22), col(20), 1.0, None, ALU.add))
                        y_start(0)
                    if k >= LAG:
                        y_level(0, k - LAG)
                    if k < N2[0]:
                        blur_level(1, k)
                blur_start(2)
                for k in range(N2[1]):
                    blur_level(2, k)
                nc.vector.memset(col(62), 0.0).then_inc(xlast_free, 1)
                v.wait_ge(xlast_free, i + 2)
                for l in range(1, LEVELS):
                    y_start(l)
                    for k in range(N2[l]):
                        y_level(l, k)
                v.wait_ge(y23_ready, i * 2 + 2)
                carry_wait()
                for k in range(5):
                    last = nc.vector.bn_aggr(moments[:, 2 + k, :], ystats[k][:])
                link(last)
                mean, var = moments[:, 2:7, 0], moments[:, 2:7, 1]
                weight = consts[:, K_REGION:K_REGION + 5]
                link(nc.vector.tensor_tensor(col(30, 5), mean, mean, ALU.mult))
                link(nc.vector.tensor_tensor(col(30, 5), col(30, 5), var, ALU.add))
                link(nc.vector.tensor_tensor(col(30, 5), col(30, 5), weight, ALU.mult))
                link(nc.vector.tensor_tensor(col(35, 5), mean, weight, ALU.mult))
                link(nc.vector.tensor_reduce(col(14), col(35, 5), AX.X, ALU.add))
                link(nc.vector.tensor_reduce(col(15), col(30, 5), AX.X, ALU.add))
                link(nc.vector.tensor_scalar(col(16), consts[:, K_LOWER:K_LOWER + 1], 1.0, col(21), ALU.add, ALU.mult))
                link(nc.vector.tensor_tensor(col(17), col(12), col(22), ALU.mult))
                link(nc.vector.tensor_tensor(col(18), col(16), col(17), ALU.add))
                link(nc.vector.tensor_tensor(col(0), col(14), col(18), ALU.add))
                link(nc.vector.scalar_tensor_tensor(out=col(18), in0=col(17), scalar=2.0, in1=col(16),
                                                    op0=ALU.mult, op1=ALU.add))
                link(nc.vector.tensor_tensor(col(18), col(18), col(21), ALU.mult))
                link(nc.vector.scalar_tensor_tensor(out=col(19), in0=col(13), scalar=col(22), in1=col(22),
                                                    op0=ALU.mult, op1=ALU.mult))
                link(nc.vector.tensor_tensor(col(18), col(18), col(19), ALU.add))
                nc.vector.tensor_tensor(col(1), col(15), col(18), ALU.add).then_inc(partial_ready, 1)
                total(i * 2 + 2, col(7), col(25), col(26))
                sc = scal[:, bass.ds(i, 1), :].rearrange("p o k -> p (o k)")
                link(nc.vector.tensor_tensor(sc[:, 0:1], col(25), col(22), ALU.mult))
                link(nc.vector.tensor_tensor(col(8), col(21), col(7), ALU.subtract))
                link(nc.vector.tensor_tensor(sc[:, 1:2], col(8), col(25), ALU.mult))
                link(nc.vector.tensor_copy(sc[:, 2:3], col(25)))
                link(nc.vector.scalar_tensor_tensor(out=sc[:, 3:4], in0=col(7), scalar=-1.0, in1=col(25),
                                                    op0=ALU.mult, op1=ALU.mult))
                nc.vector.tensor_tensor(sc[:, 4:5], col(7), biases[:], ALU.add).then_inc(scal_ready, 1)
                v.wait_ge(centre_ready, i + 1)
                nc.vector.scalar_tensor_tensor(out=w_sum[:], in0=eyes[:], scalar=col(26), in1=w_centre[:],
                                               op0=ALU.mult, op1=ALU.add).then_inc(w_sum_ready, 1)
                assert steps[1] == STEPS_IMAGE, steps

        def load_row(queue, done, i, g, s, r, upper):
            rows = bass.ds(g * GROUP, GROUP)
            src = x[i].rearrange("c (b r) w -> c r b w", r=Q)[:, r, rows, :]
            if upper:
                ysrc = y_quarter[i].rearrange("c (b r) w -> c r b w", r=Q)[:, r, rows, :]
                queue.dma_start(raw[r:P:Q, s, :, 0:WQ], ysrc).then_inc(done, 16)
                queue.dma_start(raw[r:P:Q, s, :, WQ:W], src[:, :, WQ:W]).then_inc(done, 16)
            else:
                queue.dma_start(raw[r:P:Q, s, :, :], src).then_inc(done, 32)

        @block.scalar
        def _(act):
            def load(i, g, s, upper, rows=range(Q - 1)):
                for r in rows:
                    load_row(act, raw_in[s], i, g, s, r, upper)

            def take_norm(i):
                nc.scalar.copy(norm_now[:], scal[:, bass.ds(i, 1), 0:4].rearrange("p o k -> p (o k)")
                               ).then_inc(norm_now_ready, 1)

            def take_shift(i, s):
                nc.scalar.copy(shift_now[:, s:s + 1], scal[:, bass.ds(i, 1), 4:5].rearrange("p o k -> p (o k)")
                               ).then_inc(shift_now_ready, 1)

            def prepare(i, t, n, s, upper):
                act.wait_ge(norm_now_ready, i + 1)
                act.wait_ge(raw_in[s], n * (32 * (Q - 1)) + 32 * (Q - 1))
                act.wait_ge(raw3_in[s], n * 32 + 32)
                if upper:
                    nc.scalar.activation(raw[:, s, :, 0:WQ], raw[:, s, :, 0:WQ], ACT.Identity,
                                         bias=norm_now[:, 3:4], scale=norm_now[:, 2:3])
                    nc.scalar.activation(raw[:, s, :, WQ:W], raw[:, s, :, WQ:W], ACT.Identity,
                                         bias=norm_now[:, 1:2], scale=norm_now[:, 0:1]).then_inc(normed, 1)
                else:
                    nc.scalar.activation(raw[:, s, :, :], raw[:, s, :, :], ACT.Identity,
                                         bias=norm_now[:, 1:2], scale=norm_now[:, 0:1]).then_inc(normed, 1)
                act.wait_ge(normed, t + 1)

            def high_part(s):
                nc.scalar.copy(high[:, GROUP * s:GROUP * s + GROUP, 1:W + 1], raw[:, s, :, :]
                               ).then_inc(high_ready, 1)

            ABOVE = {0: ((0, 1, 2 * GROUP - 1), (1, GROUP - 1, 0)), 1: ((0, GROUP, GROUP - 1),)}
            BELOW = {0: ((0, GROUP, 1),), 1: ((0, GROUP - 1, GROUP + 1), (GROUP - 1, 1, 0))}

            def copy_halo(pieces, row, first, s, done, edge):
                for at, n, src in pieces:
                    dst = halo[first:first + 2 * C, s, at:at + n, :].bitcast(F32)
                    if edge and n == 1:
                        act.dma_start(dst, zeros[:].bitcast(F32).rearrange("p (o w) -> p o w", o=1)
                                      ).then_inc(done, 32 // len(pieces))
                    else:
                        act.dma_start(dst.rearrange("p n w -> p (n w)"),
                                      parts[row:P:Q, :, src:src + n, :].bitcast(F32)
                                      .rearrange("c t n w -> c t (n w)")
                                      ).then_inc(done, 32 // len(pieces))

            def above(s, edge=False):
                copy_halo(ABOVE[s], Q - 1, 0, s, above_in[s], edge)

            def below(s, edge=False):
                copy_halo(BELOW[s], 0, 2 * C, s, below_in[s], edge)

            def step(i, g, t, n, s, load_next=None, prepare_next=None, last=False, first_next=False):
                if prepare_next is not None or load_next is not None or not last:
                    act.wait_ge(low_ready, t + 2)
                act.wait_ge(sums_read[s], n + 1)
                below(s, edge=last)
                take_shift(i, s)
                if not (last and prepare_next is None):
                    above(1 - s, edge=last)
                if prepare_next is not None:
                    prepare_next()
                if load_next is not None:
                    load_next(range(1))
                if prepare_next is not None:
                    act.wait_ge(main_done, t + 1)
                    act.wait_ge(below_in[s], n * 32 + 32)
                    act.wait_ge(above_in[1 - s], (n + (1 if s == 0 else 2)) * 32)
                    high_part(s)
                if load_next is not None:
                    load_next(range(1, Q - 1))
                act.wait_ge(sums_ready, t + 1)
                act.wait_ge(out_stored[s], n * (16 * Q) + 16)
                act.wait_ge(shift_now_ready, t + 1)
                nc.scalar.activation(outs[:, s, :, :], sums[:, s, :, :], ACT.Identity,
                                     bias=shift_now[:, s:s + 1]).then_inc(sums_read[s], 1)

            def start_image(i):
                act.wait_ge(y_stored, i * (16 * Q) + 16 * (Q + 1))

            act.wait_ge(conv_zeroed, 1)
            start_image(0)
            load(0, 0, 0, True)
            load(0, 1, 1, True)
            act.wait_ge(scal_ready, 1)
            take_norm(0)
            for s in range(2):
                prepare(0, s, 0, s, True)
                high_part(s)
            act.wait_ge(low_ready, 1)
            above(0, edge=True)
            load(0, 2, 0, True)

            def image(i, more):
                t0, n0 = i * G, i * (G // 2)

                def pair(g, load_upper, prepare_upper):
                    for s in range(2):
                        step(i, g + s, t0 + g + s, n0 + g_half(g), s,
                             load_next=lambda rows: load(i, g + (s + 3), 1 - s, load_upper[s], rows),
                             prepare_next=lambda: prepare(i, t0 + g + (s + 2), n0 + g_half(g) + 1, s,
                                                          prepare_upper))

                def g_half(g):
                    return halves[0]

                halves = [None]
                with act.Fori(0, GQ // 2 - 2) as k:
                    halves[0] = k
                    pair(k * 2, (True, True), True)
                halves[0] = GQ // 2 - 2
                pair(GQ - 4, (True, False), True)
                with act.Fori(GQ // 2 - 1, G // 2 - 2) as k:
                    halves[0] = k
                    pair(k * 2, (False, False), False)
                for g in range(G - 4, G):
                    s = g % 2
                    t, n = t0 + g, n0 + g // 2
                    if g + 3 < G:
                        load_next = lambda rows: load(i, g + 3, 1 - s, False, rows)
                    elif more:
                        def load_next(rows):
                            if g + 3 == G and 0 in rows:
                                start_image(i + 1)
                            load(i + 1, g + 3 - G, 1 - s, True, rows)
                    else:
                        load_next = None
                    if g + 2 < G:
                        prepare_next = lambda: prepare(i, t + 2, n + 1, s, False)
                    elif more:
                        def prepare_next():
                            if g + 2 == G:
                                act.wait_ge(scal_ready, i + 2)
                                take_norm(i + 1)
                            prepare(i + 1, t + 2, n + 1, s, True)
                    else:
                        prepare_next = None
                    step(i, g, t, n, s, load_next, prepare_next, last=g == G - 1)

            if B > 1:
                with act.Fori(0, B - 1) as i:
                    image(i, True)
            image(B - 1, False)

        @block.gpsimd
        def _(pool):
            for s in range(2):
                pool.dma_start(spare[:, 2 + s:3 + s], bias.rearrange("(c o) -> c o", o=1)
                               ).then_inc(out_stored[s], 16)
            nc.gpsimd.memset(high[:].bitcast(F32), 0.0).then_inc(sums_read[0], 1)
            nc.gpsimd.memset(low[:].bitcast(F32), 0.0).then_inc(sums_read[1], 1)
            nc.gpsimd.memset(halo[:].bitcast(F32), 0.0).then_inc(centre_ready, 1)
            nc.gpsimd.memset(zeros[:].bitcast(F32), 0.0).then_inc(conv_zeroed, 1)

            def low_part(t, s):
                pool.wait_ge(high_ready, t + 1)
                blocks = slice(GROUP * s, GROUP * s + GROUP)
                nc.gpsimd.tensor_tensor(low[:, blocks, 1:W + 1], raw[:, s, :, :],
                                        high[:, blocks, 1:W + 1].bitcast(F32), ALU.subtract
                                        ).then_inc(low_ready, 1)

            def centre(i):
                nc.gpsimd.tensor_copy(w_high[:, 1, :], w_sum[:]).then_inc(centre_high_ready, 1)
                pool.wait_ge(centre_high_ready, i + 1)
                nc.gpsimd.tensor_tensor(w_low[:, 1, :], w_sum[:], w_high[:, 1, :].bitcast(F32),
                                        ALU.subtract).then_inc(centre_ready, 1)

            def store(i, g, n, s):
                pool.wait_ge(sums_read[s], n + 2)
                for r in range(Q):
                    pool.dma_start(out[i].rearrange("c (b r) w -> c r b w", r=Q)
                                   [:, r, bass.ds(g * GROUP, GROUP), :],
                                   outs[r:P:Q, s, :, :]).then_inc(out_stored[s], 16)

            def load_last_row(i, g, t, s, upper):
                if t is not None:
                    pool.wait_ge(low_ready, t - 1)
                load_row(pool, raw3_in[s], i, g, s, Q - 1, upper)

            pool.wait_ge(y_stored, 16 * (Q + 1))
            load_last_row(0, 0, None, 0, True)
            load_last_row(0, 1, None, 1, True)
            low_part(0, 0)
            load_last_row(0, 2, 2, 0, True)
            pool.wait_ge(w_sum_ready, 1)
            low_part(1, 1)
            centre(0)

            def image(i, more):
                t0, n0 = i * G, i * (G // 2)

                def pair(k, upper):
                    for s in range(2):
                        load_last_row(i, k * 2 + (s + 3), t0 + k * 2 + (s + 3), 1 - s, upper[s])
                        low_part(t0 + k * 2 + (s + 2), s)
                        store(i, k * 2 + s, n0 + k, s)

                with pool.Fori(0, GQ // 2 - 2) as k:
                    pair(k, (True, True))
                pair(GQ // 2 - 2, (True, False))
                with pool.Fori(GQ // 2 - 1, G // 2 - 2) as k:
                    pair(k, (False, False))
                for g in range(G - 4, G):
                    s = g % 2
                    if g + 3 < G:
                        load_last_row(i, g + 3, t0 + g + 3, 1 - s, False)
                    elif more:
                        if g + 3 == G:
                            pool.wait_ge(y_stored, (i + 1) * (16 * Q) + 16 * (Q + 1))
                        load_last_row(i + 1, g + 3 - G, t0 + g + 3, 1 - s, True)
                    if g + 1 == G and more:
                        pool.wait_ge(w_sum_ready, i + 2)
                    if g + 2 < G or more:
                        low_part(t0 + g + 2, s)
                    if g + 1 == G and more:
                        centre(i + 1)
                    store(i, g, n0 + g // 2, s)

            if B > 1:
                with pool.Fori(0, B - 1) as i:
                    image(i, True)
            image(B - 1, False)
            for s in range(2):
                pool.wait_ge(out_stored[s], 16 * Q * B * G // 2 + 16)

        @block.tensor
        def _(pe):
            def sum_partitions(n):
                pe.wait_ge(partial_ready, n + 1)
                nc.tensor.matmul(sums[:, 0, 0, 0:2], groups[:], small[:, 0:2], start=True,
                                 stop=True).then_inc(total_ready, 1)

            def group(i, t, n, s, totals):
                if s == 0:
                    pe.wait_ge(total_read, totals)
                pe.wait_ge(low_ready, t + 1)
                pe.wait_ge(sums_read[s], n + 1)
                for k, (kx, weights, parts) in enumerate(
                        (kx, wgt, prt) for kx in (0, 2, 1)
                        for wgt, prt in ((w_high, high), (w_low, high), (w_high, low))):
                    if kx == 1:
                        pe.wait_ge(centre_ready, i + 2)
                    for j in range(GROUP):
                        mm = nc.tensor.matmul(sums[:, s, j, :], weights[:, kx, :],
                                              parts[:, GROUP * s + j, kx:kx + W],
                                              start=k == 0, stop=False)
                mm.then_inc(main_done, 1)
                pe.wait_ge(above_in[s], n * 32 + 32)
                pe.wait_ge(below_in[s], n * 32 + 32)
                for kx in range(3):
                    for weights in (wt_high, wt_low):
                        for j in range(GROUP):
                            mm = nc.tensor.matmul(sums[:, s, j, :], weights[:, kx, :],
                                                  halo[:, s, j, kx:kx + W], start=False,
                                                  stop=kx == 2 and weights is wt_low)
                mm.then_inc(sums_ready, 1)

            def image(i, more):
                t0, n0 = i * G, i * (G // 2)
                with pe.Fori(0, XSTAT_AT // 2) as k:
                    for s in range(2):
                        group(i, t0 + k * 2 + s, n0 + k, s, i * 2 + 2)
                if more:
                    pe.wait_ge(sums_read[0], n0 + (XSTAT_AT // 2 + 1))
                    sum_partitions(i * 2 + 2)
                with pe.Fori(XSTAT_AT // 2, YSTAT_AT // 2) as k:
                    for s in range(2):
                        group(i, t0 + k * 2 + s, n0 + k, s, i * 2 + (3 if more else 2))
                if more:
                    pe.wait_ge(sums_read[0], n0 + (YSTAT_AT // 2 + 1))
                    sum_partitions(i * 2 + 3)
                with pe.Fori(YSTAT_AT // 2, G // 2) as k:
                    for s in range(2):
                        group(i, t0 + k * 2 + s, n0 + k, s, i * 2 + (4 if more else 2))

            pe.wait_ge(consts_in, 16 * (3 + Q))
            sum_partitions(0)
            pe.wait_ge(total_read, 1)
            sum_partitions(1)
            pe.wait_ge(total_read, 2)
            if B > 1:
                with pe.Fori(0, B - 1) as i:
                    image(i, True)
            image(B - 1, False)


STEPS_CHUNKS = 8
STEPS_IMAGE = 288


def shape_constants(H):
    q = np.arange(P) % Q
    lower = (q >= 2).astype(np.float32)
    cols = [lower, (q > 0).astype(np.float32)]
    cols += [np.full(P, 1 / 4) * lower, np.full(P, 1 / 4), np.full(P, 1 / 16) * lower,
             np.full(P, 1 / 16), np.full(P, 1 / 32)]
    for l in range(LEVELS):
        for r in range(H // Q >> (l + 1)):
            cols.append(np.where((q == 0) & (r == 0), E0[l] * E0[l], E0[l]) - 1.0)
    cols += [(q == 0).astype(np.float32), (np.arange(P) % 2 == 0).astype(np.float32)]
    return np.stack(cols, 1).astype(np.float32)


def kernel(x, L1_conv_weight, L1_conv_bias):
    import concourse.bacc as _bacc
    from concourse.bass_utils import run_bass_kernel_spmd as _run

    x = np.ascontiguousarray(x)
    p = np.arange(P)
    arrays = {
        "x": x,
        "w_taps": np.ascontiguousarray(np.transpose(L1_conv_weight, (1, 2, 3, 0))),
        "bias": np.ascontiguousarray(L1_conv_bias),
        "same_group": (p[:, None] // (2 * Q) == p[None, :] // (2 * Q)).astype(np.float32),
        "eye": np.eye(P, dtype=np.float32),
        "shape_consts": shape_constants(x.shape[2]),
    }
    nc = _bacc.Bacc("TRN2", target_bir_lowering=False, num_devices=1)
    args = [nc.dram_tensor(n, a.shape, mybir.dt.from_np(a.dtype), kind="ExternalInput").ap()
            for n, a in arrays.items()]
    args.append(nc.dram_tensor("out", x.shape, F32, kind="ExternalOutput").ap())
    group_norm_pyramid_conv(nc, *args)
    r = _run(nc, [arrays], core_ids=[0])
    return r.results[0]["out"]
```

```python
from contextlib import ExitStack

import numpy as np

import concourse.bass as bass
from concourse import mybir

ALU = mybir.AluOpType
ACT = mybir.ActivationFunctionType
AX = mybir.AxisListType
F32 = mybir.dt.float32
F32R = mybir.dt.float32r
I32 = mybir.dt.int32

P = 128
Q = 4
EPS = 1e-5
PAD = 2
GROUP = 4
LEVELS = 3
E0 = (0.75, 0.625, 0.5625)
RSQRT_SEED = 0x5F3759DF
NEWTON_STEPS = 4
CHUNK = 4
MCHUNK = 8
COL_LOWER, COL_BELOW, COL_REGION, COL_EDGE = 0, 1, 2, 7


def group_norm_pyramid_conv(nc, x, w_taps, bias, same_group, eye, shape_consts, out):
    B, C, H, W = x.shape
    assert C * Q == P and H == W and w_taps.shape[0] == C
    ROWS = H // Q
    N1 = ROWS // CHUNK
    WQ = W // 2
    LR = [ROWS >> (l + 1) for l in range(LEVELS)]
    LW = [W >> (l + 1) for l in range(LEVELS)]
    N2 = [r // MCHUNK for r in LR]
    NM = sum(N2)
    NA = N1 + NM
    assert NA % 2 == 0 and all(n % 2 == 0 for n in N2) and N1 % 2 == 0
    GR = GROUP * Q
    G = H // GR
    GQ = G // 2
    WP = W + 2
    GN = float(2 * H * W)
    UNIT = float(ROWS * WQ)
    SLOT = CHUNK * (W + 2 * PAD)
    STORE1 = 16 * (1 + Q // 2)
    LAG = 3
    XSTAT_AT, YSTAT_AT = G - 14, G - 6

    y_quarter = nc.dram_tensor("y_quarter", (B, C, H // 2, WQ), F32, kind="Internal").ap()

    with ExitStack() as ctx:
        def sb(name, shape, dt=F32):
            return ctx.enter_context(nc.sbuf_tensor(name, shape, dt))

        def sem(name):
            return ctx.enter_context(nc.semaphore(name))

        xa = sb("xa", [P, 2, SLOT])
        xlast = sb("xlast", [P, W + PAD])
        hblur = sb("hblur", [P, 5 * WQ])
        level = [sb(f"level{l}", [P, LR[l], LW[l] + PAD]) for l in range(LEVELS)]
        xstats = sb("xstats", [P, 2, N1 * 2, 6])
        ystats = [sb(f"ystats{k}", [P, n, 6]) for k, n in enumerate((16, 16, 4, 4, 2))]
        moments = sb("moments", [P, 7, 2])
        xsums = sb("xsums", [P, 4, N1])
        minus_shift = sb("minus_shift", [P, 1])
        small = sb("small", [P, 64])
        consts = sb("consts", [P, shape_consts.shape[1]])
        groups = sb("groups", [P, P])
        eyes = sb("eyes", [P, P])
        scal = sb("scal", [P, B, 8])
        norm_now = sb("norm_now", [P, 4])
        shift_now = sb("shift_now", [P, 2])
        raw = sb("raw", [P, 2, GROUP, W])
        parts = sb("parts", [P, 2, 2 * GROUP, WP], F32R)
        halo = sb("halo", [P, 2, GROUP, WP], F32R)
        zeros = sb("zeros", [2 * C, WP], F32R)
        outs = sb("outs", [P, 2, GROUP, W])
        w_high = sb("w_high", [P, 3, P], F32R)
        w_low = sb("w_low", [P, 3, P], F32R)
        wt_high = sb("wt_high", [P, 3, P], F32R)
        wt_low = sb("wt_low", [P, 3, P], F32R)
        w_centre = sb("w_centre", [P, P])
        biases = sb("biases", [P, 1])
        spare = sb("spare", [C, 4])
        w_sum = sb("w_sum", [P, P])
        sums = ctx.enter_context(nc.psum_tensor("sums", [P, 2, GROUP, W], F32))

        consts_in = sem("consts_in")
        tables_in = sem("tables_in")
        weights_zeroed = sem("weights_zeroed")
        weights_in = sem("weights_in")
        weights_high = sem("weights_high")
        weights_low = sem("weights_low")
        weights_split = sem("weights_split")
        centre_in = sem("centre_in")
        conv_zeroed = sem("conv_zeroed")
        xa_in = [sem(f"xa_in{s}") for s in range(2)]
        xa_free = [sem(f"xa_free{s}") for s in range(2)]
        xlast_in = sem("xlast_in")
        x_summed = sem("x_summed")
        xlast_free = sem("xlast_free")
        dve = sem("dve")
        y1_ready = sem("y1_ready")
        y23_ready = sem("y23_ready")
        y1_stored = sem("y1_stored")
        y2_stored = sem("y2_stored")
        y_stored = sem("y_stored")
        partial_ready = sem("partial_ready")
        total_ready = sem("total_ready")
        total_read = sem("total_read")
        scal_ready = sem("scal_ready")
        w_sum_ready = sem("w_sum_ready")
        centre_high_ready = sem("centre_high_ready")
        centre_ready = sem("centre_ready")
        raw_in = [sem(f"raw_in{s}") for s in range(2)]
        raw3_in = [sem(f"raw3_in{s}") for s in range(2)]
        norm_now_ready = sem("norm_now_ready")
        shift_now_ready = sem("shift_now_ready")
        normed = sem("normed")
        high_ready = sem("high_ready")
        low_ready = sem("low_ready")
        above_in = [sem(f"above_in{s}") for s in range(2)]
        below_in = [sem(f"below_in{s}") for s in range(2)]
        main_done = sem("main_done")
        sums_ready = sem("sums_ready")
        sums_read = [sem(f"sums_read{s}") for s in range(2)]
        out_stored = [sem(f"out_stored{s}") for s in range(2)]

        high, low = parts[:, 0], parts[:, 1]

        wm = [outs[:, 0, k, 0:3 * P].rearrange("p (k o) -> p k o", k=3) for k in range(2)]
        LEFT, RIGHT = slice(PAD, PAD + WQ), slice(PAD + WQ, PAD + W)

        def x_rows(slot):
            return xa[:, slot, :].rearrange("p (r w) -> p r w", r=CHUNK)

        def m_rows(slot, width):
            return xa[:, slot, :].rearrange("p (r w) -> p r w", r=MCHUNK)[:, :, PAD:PAD + width]

        def store_y1(sp, i, k):
            rows = slice(MCHUNK * k, MCHUNK * k + MCHUNK)
            half = LW[1]
            sp.wait_ge(y1_ready, i * N2[0] + (k + 1))
            sp.dma_start(y_quarter[i].rearrange("c (q r) w -> (c q) r w", q=Q)[:, rows, half:],
                         level[0][:, rows, PAD + half:PAD + WQ]).then_inc(y1_stored, 16)
            for q in range(Q // 2, Q):
                sp.dma_start(y_quarter[i].rearrange("c (q r) w -> c q r w", q=Q)[:, q, rows, 0:half],
                             level[0][q:P:Q, rows, PAD:PAD + half]).then_inc(y1_stored, 16)

        def store_level(sp, i, l, done):
            for q in reversed(range(Q)):
                sp.dma_start(y_quarter[i, :, q * LR[l]:(q + 1) * LR[l], 0:LW[l]],
                             level[l][q:P:Q, :, PAD:PAD + LW[l]]).then_inc(done, 16)

        block = ctx.enter_context(nc.Block())

        @block.sync
        def _(sp):
            for k, done in enumerate((y1_stored, y_stored)):
                sp.dma_start(spare[:, k:k + 1], bias.rearrange("(c o) -> c o", o=1)).then_inc(done, 16)
            sp.dma_start(consts[:], shape_consts).then_inc(consts_in, 16)
            with sp.Fori(0, B) as i:
                rows = x[i].rearrange("c (q r) w -> (c q) r w", q=Q)
                chunks = x[i].rearrange("c (q k s r) w -> (c q) k s r w", q=Q, s=2, r=CHUNK)
                sp.wait_ge(xlast_free, i + 1)
                sp.dma_start(xlast[:, PAD:PAD + W], rows[:, ROWS - 1, :]).then_inc(xlast_in, 16)
                with sp.Fori(0, N1 // 2) as k:
                    for s in range(2):
                        sp.wait_ge(xa_free[s], i * (NA // 2) + k + 1)
                        sp.dma_start(x_rows(s)[:, :, PAD:PAD + W],
                                     chunks[:, bass.ds(k, 1), s].rearrange("p o r w -> p (o r) w")
                                     ).then_inc(xa_in[s], 16 * Q)
                done = N1
                for l in range(LEVELS):
                    part = x[i, :, 0:H >> (l + 1), 0:LW[l]].rearrange("c (q r) w -> c q r w", q=Q)
                    for k in range(N2[l]):
                        s = k % 2
                        sp.wait_ge(xa_free[s], i * (NA // 2) + (done // 2 + k // 2 + 1))
                        for q in reversed(range(Q)):
                            left = LW[1] if l == 0 and q < Q // 2 else 0
                            sp.dma_start(m_rows(s, LW[l])[q:P:Q, :, left:],
                                         part[:, q, MCHUNK * k:MCHUNK * k + MCHUNK, left:]
                                         ).then_inc(xa_in[s], 16)
                        if l == 0 and k >= 2:
                            store_y1(sp, i, k - 2)
                    if l == 0:
                        store_y1(sp, i, N2[0] - 2)
                        store_y1(sp, i, N2[0] - 1)
                    done += N2[l]
                sp.wait_ge(y1_stored, i * (STORE1 * N2[0]) + (STORE1 * N2[0] + 16))
                sp.wait_ge(y23_ready, i * 2 + 1)
                store_level(sp, i, 1, y2_stored)
                sp.wait_ge(y23_ready, i * 2 + 2)
                sp.wait_ge(y2_stored, i * (16 * Q) + 16 * Q)
                store_level(sp, i, 2, y_stored)
            sp.wait_ge(y_stored, 16 * Q * B + 16)

        @block.vector
        def _(v):
            steps = [0, 0]

            def link(ins):
                steps[1] += 1
                ins.then_inc(dve, 1)
                v.wait_ge(dve, steps[0] + steps[1])

            one = shape_consts.shape[1] - 2

            def col(n, width=1):
                return small[:, n:n + width]

            def carry_wait():
                nc.vector.memset(col(63), 0.0)

            def blur(src, n, width, dst, between=lambda k: None):
                def link(ins, k):
                    steps[1] += 1
                    ins.then_inc(dve, 1)
                    between(k)
                    v.wait_ge(dve, steps[0] + steps[1])

                h = hblur[:, 0:(n + 1) * width].rearrange("p (r w) -> p r w", w=width)
                left, mid = src[:, :, 1:1 + 2 * width:2], src[:, :, 2:2 + 2 * width:2]
                right = src[:, :, 3:2 + 2 * width:2]
                link(nc.vector.tensor_tensor(h[:, 1:n + 1, :], left, right, ALU.add), 0)
                link(nc.vector.scalar_tensor_tensor(out=h[:, 1:n + 1, :], in0=mid, scalar=2.0,
                                                    in1=h[:, 1:n + 1, :], op0=ALU.mult, op1=ALU.add), 1)
                link(nc.vector.tensor_tensor(dst, h[:, 0:n - 1:2, :], h[:, 2:n + 1:2, :], ALU.add), 2)
                nc.vector.scalar_tensor_tensor(out=dst, in0=h[:, 1:n:2, :], scalar=2.0, in1=dst,
                                               op0=ALU.mult, op1=ALU.add)
                link(nc.vector.tensor_copy(h[:, 0, :], h[:, n, :]), 3)

            def blur_last_row(src, width):
                shift = [max(p - 1, 0) for p in range(32)]
                carry_wait()
                link(nc.vector.stream_shuffle(src, src, shift))
                h = hblur[:, 0:width]
                link(nc.vector.tensor_tensor(h, src[:, 1:1 + 2 * width:2], src[:, 3:2 + 2 * width:2], ALU.add))
                link(nc.vector.scalar_tensor_tensor(out=h, in0=src[:, 2:2 + 2 * width:2], scalar=2.0,
                                                    in1=h, op0=ALU.mult, op1=ALU.add))
                link(nc.vector.tensor_scalar(h, h, consts[:, COL_BELOW:COL_BELOW + 1], None, ALU.mult))

            def rsqrt(dst, var, t0, t1):
                link(nc.vector.tensor_scalar(t0.bitcast(I32), var.bitcast(I32), 1, None,
                                             ALU.arith_shift_right))
                link(nc.vector.tensor_scalar(dst.bitcast(I32), t0.bitcast(I32), -1.0,
                                             float(RSQRT_SEED), ALU.mult, ALU.add))
                for _ in range(NEWTON_STEPS):
                    link(nc.vector.scalar_tensor_tensor(out=t0, in0=dst, scalar=dst, in1=var,
                                                        op0=ALU.mult, op1=ALU.mult))
                    link(nc.vector.tensor_scalar(t1, t0, -0.5, 1.5, ALU.mult, ALU.add))
                    link(nc.vector.tensor_tensor(dst, dst, t1, ALU.mult))


            def total(n_done, mean, r, sigma):
                v.wait_ge(total_ready, n_done)
                nc.vector.tensor_scalar(col(2, 2), sums[:, 0, 0, 0:2], UNIT / GN, None,
                                        ALU.mult).then_inc(total_read, 1)
                v.wait_ge(total_read, n_done)
                link(nc.vector.tensor_copy(mean, col(2)))
                link(nc.vector.tensor_tensor(col(4), col(2), col(2), ALU.mult))
                link(nc.vector.tensor_tensor(col(4), col(3), col(4), ALU.subtract))
                link(nc.vector.tensor_scalar(col(4), col(4), 0.0, EPS, ALU.max, ALU.add))
                rsqrt(r, col(4), col(5), col(6))
                link(nc.vector.tensor_tensor(sigma, col(4), r, ALU.mult))

            for s in range(2):
                nc.vector.memset(x_rows(s)[:, :, 0:PAD], 0.0)
                nc.vector.memset(x_rows(s)[:, :, PAD + W:], 0.0)
            nc.vector.memset(xlast[:, 0:PAD], 0.0)
            for l in range(LEVELS):
                nc.vector.memset(level[l][:, :, 0:PAD], 0.0)
            nc.vector.memset(small[:, 0:16], 0.0).then_inc(xa_free[0], 1)
            nc.vector.memset(small[:, 16:32], 0.0).then_inc(xa_free[1], 1)
            nc.vector.memset(small[:, 32:64], 0.0).then_inc(xlast_free, 1)
            for s in range(2):
                v.wait_ge(xa_free[s], 1)
            v.wait_ge(xlast_free, 1)
            v.wait_ge(consts_in, 16)

            def image(i, base, alone):
                steps[0], steps[1] = base, 0
                v.wait_ge(y1_stored, i * (STORE1 * N2[0]) + 16)
                v.wait_ge(y_stored, i * (16 * Q) + 16)
                v.wait_ge(xlast_in, i * 16 + 16)
                blur_last_row(xlast[:, 0:PAD + W], WQ)
                before = steps[1]
                carry_wait()
                with v.Fori(0, N1 // 2) as k:
                    steps[0], steps[1] = base + k * STEPS_CHUNKS + before, 0
                    for s in range(2):
                        v.wait_ge(xa_in[s], i * (8 * NA * Q) + k * (16 * Q) + 16 * Q)

                        def stats(n):
                            if alone:
                                if n == CHUNK - 1:
                                    v.wait_ge(x_summed, k * 2 + (s + 2))
                                    nc.vector.memset(col(61), 0.0).then_inc(xa_free[s], 1)
                                return
                            half, pair = divmod(n, CHUNK // 2)
                            ins = nc.vector.bn_stats(
                                xstats[:, half, bass.ds(k * CHUNK + (s * CHUNK // 2 + pair), 1), :]
                                .rearrange("p o k -> p (o k)"),
                                x_rows(s)[:, 2 * pair:2 * pair + 2, (LEFT, RIGHT)[half]])
                            if n == CHUNK - 1:
                                ins.then_inc(xa_free[s], 1)

                        blur(x_rows(s), CHUNK, WQ,
                             level[0][:, bass.ds(k * CHUNK + s * CHUNK // 2, CHUNK // 2), PAD:PAD + WQ],
                             between=stats)
                    assert steps[1] == STEPS_CHUNKS, steps
                steps[0], steps[1] = base, before + STEPS_CHUNKS * (N1 // 2)
                v.wait_ge(xa_free[1], i * (NA // 2) + (N1 // 2 + 1))
                carry_wait()
                if alone:
                    link(nc.vector.tensor_reduce(col(40, 4), xsums[:], AX.X, ALU.add))
                    link(nc.vector.tensor_scalar(col(40, 4), col(40, 4), 1 / UNIT, None, ALU.mult))
                    link(nc.vector.tensor_tensor(col(44, 2), col(40, 2), col(40, 2), ALU.mult))
                    link(nc.vector.tensor_tensor(moments[:, 0:2, 1], col(42, 2), col(44, 2),
                                                 ALU.subtract))
                    link(nc.vector.tensor_scalar(moments[:, 0:2, 0], col(40, 2), minus_shift[:],
                                                 None, ALU.subtract))
                else:
                    nc.vector.bn_aggr(moments[:, 0, :], xstats[:, 0, :, :])
                    link(nc.vector.bn_aggr(moments[:, 1, :], xstats[:, 1, :, :]))
                mean, var = moments[:, 0:2, 0], moments[:, 0:2, 1]
                link(nc.vector.tensor_tensor(col(10, 2), mean, mean, ALU.mult))
                link(nc.vector.tensor_tensor(col(10, 2), col(10, 2), var, ALU.add))
                link(nc.vector.tensor_tensor(col(0), moments[:, 0, 0:1], moments[:, 1, 0:1], ALU.add))
                nc.vector.tensor_tensor(col(1), col(10), col(11), ALU.add).then_inc(partial_ready, 1)
                link(nc.vector.scalar_tensor_tensor(out=col(12), in0=moments[:, 0, 0:1],
                                                    scalar=consts[:, COL_LOWER:COL_LOWER + 1],
                                                    in1=moments[:, 1, 0:1], op0=ALU.mult, op1=ALU.add))
                link(nc.vector.scalar_tensor_tensor(out=col(13), in0=col(10),
                                                    scalar=consts[:, COL_LOWER:COL_LOWER + 1],
                                                    in1=col(11), op0=ALU.mult, op1=ALU.add))
                def blur_start(l):
                    last = xlast[:, 0:PAD + LW[l - 1]]
                    link(nc.vector.tensor_copy(last[:, PAD:], level[l - 1][:, LR[l - 1] - 1, PAD:]))
                    blur_last_row(last, LW[l])

                def blur_level(l, k):
                    blur(level[l - 1][:, MCHUNK * k:MCHUNK * k + MCHUNK, :], MCHUNK, LW[l],
                         level[l][:, MCHUNK // 2 * k:MCHUNK // 2 * (k + 1), PAD:])

                def y_start(l):
                    link(nc.vector.tensor_scalar(col(23), col(20), 16.0 ** -(l + 1), None, ALU.mult))
                    link(nc.vector.tensor_scalar(col(24), col(21), E0[l] - 1.0, None, ALU.mult))
                    link(nc.vector.tensor_tensor(col(24), col(24), consts[:, one:one + 1], ALU.mult))

                def y_level(l, k):
                    seen = (N1 + sum(N2[:l])) // 2 + k // 2
                    edge = COL_EDGE + sum(LR[:l]) + MCHUNK * k
                    s = k % 2
                    y = level[l][:, MCHUNK * k:MCHUNK * k + MCHUNK, PAD:]
                    v.wait_ge(xa_in[s], i * (8 * NA * Q) + 16 * Q * (seen + 1))
                    link(nc.vector.scalar_tensor_tensor(out=y, in0=y, scalar=col(23),
                                                        in1=m_rows(s, LW[l]),
                                                        op0=ALU.mult, op1=ALU.add))
                    nc.vector.tensor_scalar(y, y, col(21), None, ALU.add).then_inc(xa_free[s], 1)
                    v.wait_ge(xa_free[s], i * (NA // 2) + (seen + 2))
                    ec = consts[:, edge:edge + MCHUNK].rearrange("p (r o) -> p r o", o=1)
                    last = nc.vector.scalar_tensor_tensor(out=y[:, :, 0:1], in0=ec, scalar=col(21),
                                                          in1=y[:, :, 0:1], op0=ALU.mult, op1=ALU.add)
                    if k == 0:
                        link(last)
                        last = nc.vector.tensor_scalar(y[:, 0, 1:], y[:, 0, 1:], col(24), None, ALU.add)
                    if l == 0:
                        last.then_inc(y1_ready, 1)
                        v.wait_ge(y1_ready, i * N2[0] + (k + 1))
                    else:
                        link(last)
                    if l < LEVELS - 1:
                        n = 512 // (LW[l] // 2)
                        for j in range(MCHUNK // n):
                            for half in range(2):
                                last = nc.vector.bn_stats(
                                    ystats[2 * l + half][:, k * (MCHUNK // n) + j, :],
                                    y[:, n * j:n * j + n, half * LW[l] // 2:(half + 1) * LW[l] // 2])
                    else:
                        last = nc.vector.bn_stats(ystats[2 * l][:, k, :], y)
                    if l and k == N2[l] - 1:
                        last.then_inc(y23_ready, 1)

                blur_start(1)
                for k in range(N2[0] + LAG):
                    if k == LAG:
                        total(i * 2 + 1, col(7), col(20), col(8))
                        link(nc.vector.scalar_tensor_tensor(out=col(21), in0=col(7), scalar=-1.0,
                                                            in1=col(20), op0=ALU.mult, op1=ALU.mult))
                        link(nc.vector.tensor_scalar(col(22), col(20), 1.0, None, ALU.add))
                        y_start(0)
                    if k >= LAG:
                        y_level(0, k - LAG)
                    if k < N2[0]:
                        blur_level(1, k)
                blur_start(2)
                for k in range(N2[1]):
                    blur_level(2, k)
                nc.vector.memset(col(62), 0.0).then_inc(xlast_free, 1)
                v.wait_ge(xlast_free, i + 2)
                for l in range(1, LEVELS):
                    y_start(l)
                    for k in range(N2[l]):
                        y_level(l, k)
                v.wait_ge(y23_ready, i * 2 + 2)
                carry_wait()
                for k in range(5):
                    last = nc.vector.bn_aggr(moments[:, 2 + k, :], ystats[k][:])
                link(last)
                mean, var = moments[:, 2:7, 0], moments[:, 2:7, 1]
                weight = consts[:, COL_REGION:COL_REGION + 5]
                link(nc.vector.tensor_tensor(col(30, 5), mean, mean, ALU.mult))
                link(nc.vector.tensor_tensor(col(30, 5), col(30, 5), var, ALU.add))
                link(nc.vector.tensor_tensor(col(30, 5), col(30, 5), weight, ALU.mult))
                link(nc.vector.tensor_tensor(col(35, 5), mean, weight, ALU.mult))
                link(nc.vector.tensor_reduce(col(14), col(35, 5), AX.X, ALU.add))
                link(nc.vector.tensor_reduce(col(15), col(30, 5), AX.X, ALU.add))
                link(nc.vector.tensor_scalar(col(16), consts[:, COL_LOWER:COL_LOWER + 1], 1.0, col(21), ALU.add, ALU.mult))
                link(nc.vector.tensor_tensor(col(17), col(12), col(22), ALU.mult))
                link(nc.vector.tensor_tensor(col(18), col(16), col(17), ALU.add))
                link(nc.vector.tensor_tensor(col(0), col(14), col(18), ALU.add))
                link(nc.vector.scalar_tensor_tensor(out=col(18), in0=col(17), scalar=2.0, in1=col(16),
                                                    op0=ALU.mult, op1=ALU.add))
                link(nc.vector.tensor_tensor(col(18), col(18), col(21), ALU.mult))
                link(nc.vector.scalar_tensor_tensor(out=col(19), in0=col(13), scalar=col(22), in1=col(22),
                                                    op0=ALU.mult, op1=ALU.mult))
                link(nc.vector.tensor_tensor(col(18), col(18), col(19), ALU.add))
                nc.vector.tensor_tensor(col(1), col(15), col(18), ALU.add).then_inc(partial_ready, 1)
                total(i * 2 + 2, col(7), col(25), col(26))
                sc = scal[:, bass.ds(i, 1), :].rearrange("p o k -> p (o k)")
                link(nc.vector.tensor_tensor(sc[:, 0:1], col(25), col(22), ALU.mult))
                link(nc.vector.tensor_tensor(col(8), col(21), col(7), ALU.subtract))
                link(nc.vector.tensor_tensor(sc[:, 1:2], col(8), col(25), ALU.mult))
                link(nc.vector.tensor_copy(sc[:, 2:3], col(25)))
                link(nc.vector.scalar_tensor_tensor(out=sc[:, 3:4], in0=col(7), scalar=-1.0, in1=col(25),
                                                    op0=ALU.mult, op1=ALU.mult))
                v.wait_ge(tables_in, 16 * (2 + Q))
                nc.vector.tensor_tensor(sc[:, 4:5], col(7), biases[:], ALU.add).then_inc(scal_ready, 1)
                v.wait_ge(centre_in, 1)
                v.wait_ge(centre_ready, i + 1)
                nc.vector.scalar_tensor_tensor(out=w_sum[:], in0=eyes[:], scalar=col(26), in1=w_centre[:],
                                               op0=ALU.mult, op1=ALU.add).then_inc(w_sum_ready, 1)

            first = steps[1]
            image(0, first, True)
            first += steps[1]
            if B > 1:
                with v.Fori(1, B) as i:
                    image(i, (i - 1) * STEPS_IMAGE + first, False)
                    assert steps[1] == STEPS_IMAGE, steps

        def load_row(queue, done, i, g, s, r, upper):
            rows = bass.ds(g * GROUP, GROUP)
            src = x[i].rearrange("c (b r) w -> c r b w", r=Q)[:, r, rows, :]
            if upper:
                ysrc = y_quarter[i].rearrange("c (b r) w -> c r b w", r=Q)[:, r, rows, :]
                queue.dma_start(raw[r:P:Q, s, :, 0:WQ], ysrc).then_inc(done, 16)
                queue.dma_start(raw[r:P:Q, s, :, WQ:W], src[:, :, WQ:W]).then_inc(done, 16)
            else:
                queue.dma_start(raw[r:P:Q, s, :, :], src).then_inc(done, 32)

        @block.scalar
        def _(act):
            def load(i, g, s, upper):
                for r in range(Q - 1):
                    load_row(act, raw_in[s], i, g, s, r, upper)

            def take_norm(i):
                nc.scalar.copy(norm_now[:], scal[:, bass.ds(i, 1), 0:4].rearrange("p o k -> p (o k)")
                               ).then_inc(norm_now_ready, 1)

            def take_shift(i, s):
                nc.scalar.copy(shift_now[:, s:s + 1], scal[:, bass.ds(i, 1), 4:5].rearrange("p o k -> p (o k)")
                               ).then_inc(shift_now_ready, 1)

            def prepare(i, t, n, s, upper):
                act.wait_ge(norm_now_ready, i + 1)
                act.wait_ge(raw_in[s], n * (32 * (Q - 1)) + 32 * (Q - 1))
                act.wait_ge(raw3_in[s], n * 32 + 32)
                if upper:
                    nc.scalar.activation(raw[:, s, :, 0:WQ], raw[:, s, :, 0:WQ], ACT.Identity,
                                         bias=norm_now[:, 3:4], scale=norm_now[:, 2:3])
                    nc.scalar.activation(raw[:, s, :, WQ:W], raw[:, s, :, WQ:W], ACT.Identity,
                                         bias=norm_now[:, 1:2], scale=norm_now[:, 0:1]).then_inc(normed, 1)
                else:
                    nc.scalar.activation(raw[:, s, :, :], raw[:, s, :, :], ACT.Identity,
                                         bias=norm_now[:, 1:2], scale=norm_now[:, 0:1]).then_inc(normed, 1)
                act.wait_ge(normed, t + 1)

            def high_part(s):
                nc.scalar.copy(high[:, GROUP * s:GROUP * s + GROUP, 1:W + 1], raw[:, s, :, :]
                               ).then_inc(high_ready, 1)

            ABOVE = {0: ((0, 1, 2 * GROUP - 1), (1, GROUP - 1, 0)), 1: ((0, GROUP, GROUP - 1),)}
            BELOW = {0: ((0, GROUP, 1),), 1: ((0, GROUP - 1, GROUP + 1), (GROUP - 1, 1, 0))}

            def copy_halo(pieces, row, first, s, done, edge):
                for at, n, src in pieces:
                    dst = halo[first:first + 2 * C, s, at:at + n, :].bitcast(F32)
                    if edge and n == 1:
                        act.dma_start(dst, zeros[:].bitcast(F32).rearrange("p (o w) -> p o w", o=1)
                                      ).then_inc(done, 32 // len(pieces))
                    else:
                        act.dma_start(dst.rearrange("p n w -> p (n w)"),
                                      parts[row:P:Q, :, src:src + n, :].bitcast(F32)
                                      .rearrange("c t n w -> c t (n w)")
                                      ).then_inc(done, 32 // len(pieces))

            def above(s, edge=False):
                copy_halo(ABOVE[s], Q - 1, 0, s, above_in[s], edge)

            def below(s, edge=False):
                copy_halo(BELOW[s], 0, 2 * C, s, below_in[s], edge)

            def step(i, t, n, s, load_next, prepare_next, last=False):
                if prepare_next is not None or load_next is not None or not last:
                    act.wait_ge(low_ready, t + 2)
                act.wait_ge(sums_read[s], n + 1)
                below(s, edge=last)
                take_shift(i, s)
                if not (last and prepare_next is None):
                    above(1 - s, edge=last)
                if prepare_next is not None:
                    prepare_next()
                if prepare_next is not None:
                    act.wait_ge(main_done, t + 1)
                    act.wait_ge(below_in[s], n * 32 + 32)
                    act.wait_ge(above_in[1 - s], (n + (1 if s == 0 else 2)) * 32)
                    high_part(s)
                if load_next is not None:
                    load_next()
                act.wait_ge(sums_ready, t + 1)
                act.wait_ge(out_stored[s], n * (16 * Q) + 16)
                act.wait_ge(shift_now_ready, t + 1)
                nc.scalar.activation(outs[:, s, :, :], sums[:, s, :, :], ACT.Identity,
                                     bias=shift_now[:, s:s + 1]).then_inc(sums_read[s], 1)

            def start_image(i):
                act.wait_ge(y_stored, i * (16 * Q) + 16 * (Q + 1))

            act.dma_start(groups[:], same_group).then_inc(tables_in, 16)
            act.dma_start(eyes[:], eye).then_inc(tables_in, 16)
            for r in range(Q):
                act.dma_start(biases[r:P:Q, :], bias.rearrange("(c o) -> c o", o=1)
                              ).then_inc(tables_in, 16)
            act.wait_ge(weights_zeroed, 1)
            for r in range(Q):
                for o in range(Q):
                    if 0 <= r - o + 1 < 3:
                        act.dma_start(wm[0][r:P:Q, :, C * o:C * o + C],
                                     w_taps[:, r - o + 1]).then_inc(weights_in, 16)
            for part in range(2):
                for first, ky, o in ((0, 0, 0), (2 * C, 2, Q - 1)):
                    act.dma_start(wm[1][first + part:first + 2 * C:2, :, C * o:C * o + C],
                                 w_taps[:, ky]).then_inc(weights_in, 16)

            act.wait_ge(weights_in, 16 * 14)
            for fine, hi in ((wm[0], w_high), (wm[1], wt_high)):
                for kx in range(3):
                    f = fine[:, kx, :].rearrange("p (o c) -> p c o", o=Q)
                    h = hi[:, kx, :].rearrange("p (c o) -> p c o", o=Q)
                    nc.scalar.copy(h, f).then_inc(weights_high, 1)
            nc.scalar.copy(w_centre[:].rearrange("p (c o) -> p c o", o=Q),
                           wm[0][:, 1, :].rearrange("p (o c) -> p c o", o=Q)).then_inc(centre_in, 1)

            act.wait_ge(xa_in[0], 16 * Q)
            nc.scalar.activation(minus_shift[:], x_rows(0)[:, 0, PAD:PAD + 1], ACT.Copy,
                                 scale=-1.0).then_inc(x_summed, 1)
            with act.Fori(0, N1 // 2) as k:
                for s in range(2):
                    act.wait_ge(x_summed, k * 2 + (s + 1))
                    act.wait_ge(xa_in[s], k * (16 * Q) + 16 * Q)
                    nc.scalar.copy(shift_now[:, 0:1], minus_shift[:])
                    for n, func in enumerate((ACT.Identity, ACT.Square)):
                        for half, cols in enumerate((LEFT, RIGHT)):
                            ins = nc.scalar.activation(
                                raw[:, n, :, half * WQ:(half + 1) * WQ], x_rows(s)[:, :, cols], func,
                                bias=minus_shift[:],
                                accum_out=xsums[:, 2 * n + half, bass.ds(k * 2 + s, 1)])
                    ins.then_inc(x_summed, 1)
            act.wait_ge(x_summed, N1 + 1)

            act.wait_ge(conv_zeroed, 1)
            act.wait_ge(weights_split, 1)
            start_image(0)
            load(0, 0, 0, True)
            load(0, 1, 1, True)
            act.wait_ge(scal_ready, 1)
            take_norm(0)
            for s in range(2):
                prepare(0, s, 0, s, True)
                high_part(s)
            act.wait_ge(low_ready, 1)
            above(0, edge=True)
            load(0, 2, 0, True)

            def image(i, more):
                t0, n0 = i * G, i * (G // 2)

                def pair(k, load_upper, prepare_upper):
                    for s in range(2):
                        step(i, t0 + k * 2 + s, n0 + k, s,
                             lambda: load(i, k * 2 + (s + 3), 1 - s, load_upper[s]),
                             lambda: prepare(i, t0 + k * 2 + (s + 2), n0 + k + 1, s, prepare_upper))

                with act.Fori(0, GQ // 2 - 2) as k:
                    pair(k, (True, True), True)
                pair(GQ // 2 - 2, (True, False), True)
                with act.Fori(GQ // 2 - 1, G // 2 - 2) as k:
                    pair(k, (False, False), False)
                for g in range(G - 4, G):
                    s = g % 2
                    t, n = t0 + g, n0 + g // 2
                    if g + 3 < G:
                        load_next = lambda: load(i, g + 3, 1 - s, False)
                    elif more:
                        def load_next():
                            if g + 3 == G:
                                start_image(i + 1)
                            load(i + 1, g + 3 - G, 1 - s, True)
                    else:
                        load_next = None
                    if g + 2 < G:
                        prepare_next = lambda: prepare(i, t + 2, n + 1, s, False)
                    elif more:
                        def prepare_next():
                            if g + 2 == G:
                                act.wait_ge(scal_ready, i + 2)
                                take_norm(i + 1)
                            prepare(i + 1, t + 2, n + 1, s, True)
                    else:
                        prepare_next = None
                    step(i, t, n, s, load_next, prepare_next, last=g == G - 1)

            if B > 1:
                with act.Fori(0, B - 1) as i:
                    image(i, True)
            image(B - 1, False)

        @block.gpsimd
        def _(pool):
            nc.gpsimd.memset(outs[:, 0, 0:2, 0:3 * P], 0.0).then_inc(weights_zeroed, 1)
            for s in range(2):
                pool.dma_start(spare[:, 2 + s:3 + s], bias.rearrange("(c o) -> c o", o=1)
                               ).then_inc(out_stored[s], 16)
            nc.gpsimd.memset(high[:].bitcast(F32), 0.0).then_inc(sums_read[0], 1)
            nc.gpsimd.memset(low[:].bitcast(F32), 0.0).then_inc(sums_read[1], 1)
            nc.gpsimd.memset(halo[:].bitcast(F32), 0.0).then_inc(centre_ready, 1)
            nc.gpsimd.memset(zeros[:].bitcast(F32), 0.0).then_inc(conv_zeroed, 1)

            for part, (fine, hi, lo) in enumerate(((wm[0], w_high, w_low), (wm[1], wt_high, wt_low))):
                for kx in range(3):
                    pool.wait_ge(weights_high, 3 * part + kx + 1)
                    f = fine[:, kx, :].rearrange("p (o c) -> p c o", o=Q)
                    h = hi[:, kx, :].rearrange("p (c o) -> p c o", o=Q)
                    l = lo[:, kx, :].rearrange("p (c o) -> p c o", o=Q)
                    nc.gpsimd.tensor_tensor(l, f, h.bitcast(F32), ALU.subtract).then_inc(weights_low, 1)
            pool.wait_ge(weights_low, 6)
            pool.wait_ge(consts_in, 16)
            even = shape_consts.shape[1] - 1
            nc.gpsimd.tensor_scalar(wt_low[:], wt_low[:].bitcast(F32), consts[:, even:even + 1],
                                    None, ALU.mult).then_inc(weights_split, 1)

            def low_part(t, s):
                pool.wait_ge(high_ready, t + 1)
                blocks = slice(GROUP * s, GROUP * s + GROUP)
                nc.gpsimd.tensor_tensor(low[:, blocks, 1:W + 1], raw[:, s, :, :],
                                        high[:, blocks, 1:W + 1].bitcast(F32), ALU.subtract
                                        ).then_inc(low_ready, 1)

            def centre(i):
                nc.gpsimd.tensor_copy(w_high[:, 1, :], w_sum[:]).then_inc(centre_high_ready, 1)
                pool.wait_ge(centre_high_ready, i + 1)
                nc.gpsimd.tensor_tensor(w_low[:, 1, :], w_sum[:], w_high[:, 1, :].bitcast(F32),
                                        ALU.subtract).then_inc(centre_ready, 1)

            def store(i, g, n, s):
                pool.wait_ge(sums_read[s], n + 2)
                for r in range(Q):
                    pool.dma_start(out[i].rearrange("c (b r) w -> c r b w", r=Q)
                                   [:, r, bass.ds(g * GROUP, GROUP), :],
                                   outs[r:P:Q, s, :, :]).then_inc(out_stored[s], 16)

            def load_last_row(i, g, t, s, upper):
                if t is not None:
                    pool.wait_ge(low_ready, t - 1)
                load_row(pool, raw3_in[s], i, g, s, Q - 1, upper)

            pool.wait_ge(y_stored, 16 * (Q + 1))
            pool.wait_ge(x_summed, N1 + 1)
            load_last_row(0, 0, None, 0, True)
            load_last_row(0, 1, None, 1, True)
            low_part(0, 0)
            load_last_row(0, 2, 2, 0, True)
            pool.wait_ge(w_sum_ready, 1)
            low_part(1, 1)
            centre(0)

            def image(i, more):
                t0, n0 = i * G, i * (G // 2)

                def pair(k, upper):
                    for s in range(2):
                        load_last_row(i, k * 2 + (s + 3), t0 + k * 2 + (s + 3), 1 - s, upper[s])
                        low_part(t0 + k * 2 + (s + 2), s)
                        store(i, k * 2 + s, n0 + k, s)

                with pool.Fori(0, GQ // 2 - 2) as k:
                    pair(k, (True, True))
                pair(GQ // 2 - 2, (True, False))
                with pool.Fori(GQ // 2 - 1, G // 2 - 2) as k:
                    pair(k, (False, False))
                for g in range(G - 4, G):
                    s = g % 2
                    if g + 3 < G:
                        load_last_row(i, g + 3, t0 + g + 3, 1 - s, False)
                    elif more:
                        if g + 3 == G:
                            pool.wait_ge(y_stored, (i + 1) * (16 * Q) + 16 * (Q + 1))
                        load_last_row(i + 1, g + 3 - G, t0 + g + 3, 1 - s, True)
                    if g + 1 == G and more:
                        pool.wait_ge(w_sum_ready, i + 2)
                    if g + 2 < G or more:
                        low_part(t0 + g + 2, s)
                    if g + 1 == G and more:
                        centre(i + 1)
                    store(i, g, n0 + g // 2, s)

            if B > 1:
                with pool.Fori(0, B - 1) as i:
                    image(i, True)
            image(B - 1, False)
            for s in range(2):
                pool.wait_ge(out_stored[s], 16 * Q * B * G // 2 + 16)

        @block.tensor
        def _(pe):
            def sum_partitions(n):
                pe.wait_ge(partial_ready, n + 1)
                nc.tensor.matmul(sums[:, 0, 0, 0:2], groups[:], small[:, 0:2], start=True,
                                 stop=True).then_inc(total_ready, 1)

            def group(i, t, n, s, totals):
                if s == 0:
                    pe.wait_ge(total_read, totals)
                pe.wait_ge(low_ready, t + 1)
                pe.wait_ge(sums_read[s], n + 1)
                for k, (kx, weights, parts) in enumerate(
                        (kx, wgt, prt) for kx in (0, 2, 1)
                        for wgt, prt in ((w_high, high), (w_low, high), (w_high, low))):
                    if kx == 1:
                        pe.wait_ge(centre_ready, i + 2)
                    for j in range(GROUP):
                        mm = nc.tensor.matmul(sums[:, s, j, :], weights[:, kx, :],
                                              parts[:, GROUP * s + j, kx:kx + W],
                                              start=k == 0, stop=False)
                mm.then_inc(main_done, 1)
                pe.wait_ge(above_in[s], n * 32 + 32)
                pe.wait_ge(below_in[s], n * 32 + 32)
                for kx in range(3):
                    for weights in (wt_high, wt_low):
                        for j in range(GROUP):
                            mm = nc.tensor.matmul(sums[:, s, j, :], weights[:, kx, :],
                                                  halo[:, s, j, kx:kx + W], start=False,
                                                  stop=kx == 2 and weights is wt_low)
                mm.then_inc(sums_ready, 1)

            def image(i, more):
                t0, n0 = i * G, i * (G // 2)
                with pe.Fori(0, XSTAT_AT // 2) as k:
                    for s in range(2):
                        group(i, t0 + k * 2 + s, n0 + k, s, i * 2 + 2)
                if more:
                    pe.wait_ge(sums_read[0], n0 + (XSTAT_AT // 2 + 1))
                    sum_partitions(i * 2 + 2)
                with pe.Fori(XSTAT_AT // 2, YSTAT_AT // 2) as k:
                    for s in range(2):
                        group(i, t0 + k * 2 + s, n0 + k, s, i * 2 + (3 if more else 2))
                if more:
                    pe.wait_ge(sums_read[0], n0 + (YSTAT_AT // 2 + 1))
                    sum_partitions(i * 2 + 3)
                with pe.Fori(YSTAT_AT // 2, G // 2) as k:
                    for s in range(2):
                        group(i, t0 + k * 2 + s, n0 + k, s, i * 2 + (4 if more else 2))

            pe.wait_ge(tables_in, 16 * (2 + Q))
            sum_partitions(0)
            pe.wait_ge(total_read, 1)
            sum_partitions(1)
            pe.wait_ge(total_read, 2)
            pe.wait_ge(weights_split, 1)
            if B > 1:
                with pe.Fori(0, B - 1) as i:
                    image(i, True)
            image(B - 1, False)


STEPS_CHUNKS = 8
STEPS_IMAGE = 288


def shape_constants(H):
    q = np.arange(P) % Q
    lower = (q >= 2).astype(np.float32)
    cols = [lower, (q > 0).astype(np.float32)]
    cols += [np.full(P, 1 / 4) * lower, np.full(P, 1 / 4), np.full(P, 1 / 16) * lower,
             np.full(P, 1 / 16), np.full(P, 1 / 32)]
    for l in range(LEVELS):
        for r in range(H // Q >> (l + 1)):
            cols.append(np.where((q == 0) & (r == 0), E0[l] * E0[l], E0[l]) - 1.0)
    cols += [(q == 0).astype(np.float32), (np.arange(P) % 2 == 0).astype(np.float32)]
    return np.stack(cols, 1).astype(np.float32)


def kernel(x, L1_conv_weight, L1_conv_bias):
    import concourse.bacc as _bacc
    from concourse.bass_utils import run_bass_kernel_spmd as _run

    x = np.ascontiguousarray(x)
    p = np.arange(P)
    arrays = {
        "x": x,
        "w_taps": np.ascontiguousarray(np.transpose(L1_conv_weight, (1, 2, 3, 0))),
        "bias": np.ascontiguousarray(L1_conv_bias),
        "same_group": (p[:, None] // (2 * Q) == p[None, :] // (2 * Q)).astype(np.float32),
        "eye": np.eye(P, dtype=np.float32),
        "shape_consts": shape_constants(x.shape[2]),
    }
    nc = _bacc.Bacc("TRN2", target_bir_lowering=False, num_devices=1)
    args = [nc.dram_tensor(n, a.shape, mybir.dt.from_np(a.dtype), kind="ExternalInput").ap()
            for n, a in arrays.items()]
    args.append(nc.dram_tensor("out", x.shape, F32, kind="ExternalOutput").ap())
    group_norm_pyramid_conv(nc, *args)
    r = _run(nc, [arrays], core_ids=[0])
    return r.results[0]["out"]
```
